# Optimizing a Trainium2 kernel written in Bass

```python
import numpy as np
import jax
import jax.numpy as jnp

def _softmax(x, axis=-1):
    return jax.nn.softmax(x, axis=axis)

def _gelu(x):
    return jax.nn.gelu(x, approximate=True)

def _silu(x):
    return jax.nn.silu(x)

def _sigmoid(x):
    return jax.nn.sigmoid(x)

def _layernorm(x, axis=-1, eps=1e-05):
    m = jnp.mean(x, axis=axis, keepdims=True)
    v = jnp.var(x, axis=axis, keepdims=True)
    return (x - m) / jnp.sqrt(v + eps)

def _scatter_add(tgt, idx, src, axis=0):
    return tgt.at[idx].add(src)

def _segment_sum(src, seg, n):
    return jax.ops.segment_sum(src, seg, n)
kernel_name = 'mk_flamingo_gated_d1_seqx_r8_95f851'

def setup_inputs(seed: int=0):
    np.random.seed(seed)
    _w = jnp.asarray

    def _rec_inputs():
        import jax
        import jax.numpy as jnp
        _rk = jax.random.key(seed)
        x = -0.0003929 + 0.9999 * jax.random.normal(jax.random.fold_in(_rk, 1), (4, 512, 128), jnp.float32)
        _lenS = 512 - jax.random.randint(jax.random.fold_in(_rk, 7), (4,), 0, max(1, 512 // 4) + 1, jnp.int32)
        _lenS2 = 77 - jax.random.randint(jax.random.fold_in(_rk, 8), (4,), 0, max(1, 77 // 4) + 1, jnp.int32)
        _ctx_1024P = jax.random.normal(jax.random.fold_in(_rk, 11), (4, 16, 128), jnp.float32)
        _ctx_1024c = jax.random.dirichlet(jax.random.fold_in(_rk, 511), 0.3 * jnp.ones((16,), jnp.float32), (4, 77))
        _ctx_1024t = jnp.einsum('bsk,bkd->bsd', _ctx_1024c, _ctx_1024P)
        _ctx_1024t = _ctx_1024t * jax.lax.rsqrt(jnp.mean(jnp.square(_ctx_1024t)) + 1e-12) * 0.953939
        ctx_1024 = -3.05549e-07 + 0.0199987 * (_ctx_1024t + 0.3 * jax.random.normal(jax.random.fold_in(_rk, 611), (4, 77, 128), jnp.float32))
        _g = jax.random.normal(jax.random.fold_in(_rk, 9001), (2, 1), jnp.float32)
        _g = jnp.sign(_g) * jnp.maximum(jnp.abs(_g), 1.0) + (_g == 0) * 1.0
        g_xattn = _g[0]
        g_ffn = _g[1]
        return (x, ctx_1024, g_xattn, g_ffn)
    x, ctx_1024, g_xattn, g_ffn = _rec_inputs()

    def _L0_xattn_setup():
        import jax, jax.numpy as jnp
        import numpy as np
        E, T, H, F = (8, 256, 128, 512)
        key = jax.random.key(seed)
        k1, k2, k3 = jax.random.split(key, 3)
        x = jax.random.normal(k1, (E, T, H), dtype=jnp.float32)
        w1 = jax.random.normal(k2, (E, F, H), dtype=jnp.float32) * 0.02
        w2 = jax.random.normal(k3, (E, F, H), dtype=jnp.float32) * 0.02
        return {'x': x, 'w1': w1, 'w2': w2}
    _L0_xattn_all = _L0_xattn_setup()
    _L0_xattn_in = {k: v for k, v in _L0_xattn_all.items() if k in ()}
    del _L0_xattn_all

    def _L0_ffn_setup():
        import jax, jax.numpy as jnp
        import numpy as np
        H = 128
        M = 64
        E = 16
        TOP_K = 4
        N_GROUP = 4
        TOPK_GROUP = 2
        SCALE = 2.5
        B, S = (2, 128)

        def _gate(x2d, gate_kernel, gate_bias):
            n = x2d.shape[0]
            logits = jnp.dot(x2d.astype(jnp.float32), gate_kernel.astype(jnp.float32))
            scores = jax.nn.sigmoid(logits)
            scores_for_choice = scores + gate_bias
            group_scores = scores_for_choice.reshape(n, N_GROUP, E // N_GROUP)
            top2 = jax.lax.top_k(group_scores, k=2)[0]
            group_sum = jnp.sum(top2, axis=-1)
            group_idx = jax.lax.top_k(group_sum, k=TOPK_GROUP)[1]
            group_mask = jnp.zeros_like(group_sum).at[jnp.arange(n)[:, None], group_idx].set(1.0)
            score_mask = jnp.repeat(group_mask[:, :, None], E // N_GROUP, axis=2).reshape(n, E)
            masked_scores = jnp.where(score_mask > 0, scores_for_choice, 0.0)
            topk_weight, topk_idx = jax.lax.top_k(masked_scores, k=TOP_K)
            topk_weight = topk_weight / (jnp.sum(topk_weight, axis=-1, keepdims=True) + 1e-20)
            topk_weight = topk_weight * SCALE
            return (topk_idx, topk_weight)
        key = jax.random.key(seed)
        ks = jax.random.split(key, 9)
        sc_h = 1.0 / np.sqrt(H)
        sc_m = 1.0 / np.sqrt(M)
        return {'hidden_states': jax.random.normal(ks[0], (B, S, H), jnp.float32), 'gate_kernel': jax.random.normal(ks[1], (H, E), jnp.float32) * sc_h, 'gate_bias': jax.random.normal(ks[2], (E,), jnp.float32) * 0.01, 'w_gate': jax.random.normal(ks[3], (E, H, M), jnp.float32) * sc_h, 'w_up': jax.random.normal(ks[4], (E, H, M), jnp.float32) * sc_h, 'w_down': jax.random.normal(ks[5], (E, M, H), jnp.float32) * sc_m, 'sw_gate': jax.random.normal(ks[6], (H, 2 * M), jnp.float32) * sc_h, 'sw_up': jax.random.normal(ks[7], (H, 2 * M), jnp.float32) * sc_h, 'sw_down': jax.random.normal(ks[8], (2 * M, H), jnp.float32) * (1.0 / np.sqrt(2 * M))}
    _L0_ffn_all = _L0_ffn_setup()
    _L0_ffn_in = {k: v for k, v in _L0_ffn_all.items() if k in ('gate_kernel', 'gate_bias', 'w_gate', 'w_up', 'w_down', 'sw_gate', 'sw_up', 'sw_down')}
    del _L0_ffn_all
    return {'x': x, 'ctx_1024': ctx_1024, 'g_xattn': g_xattn, 'g_ffn': g_ffn, 'L0_ffn_gate_kernel': _L0_ffn_in['gate_kernel'], 'L0_ffn_gate_bias': _L0_ffn_in['gate_bias'], 'L0_ffn_w_gate': _L0_ffn_in['w_gate'], 'L0_ffn_w_up': _L0_ffn_in['w_up'], 'L0_ffn_w_down': _L0_ffn_in['w_down'], 'L0_ffn_sw_gate': _L0_ffn_in['sw_gate'], 'L0_ffn_sw_up': _L0_ffn_in['sw_up'], 'L0_ffn_sw_down': _L0_ffn_in['sw_down']}

def reference(x, ctx_1024, g_xattn, g_ffn, L0_ffn_gate_kernel, L0_ffn_gate_bias, L0_ffn_w_gate, L0_ffn_w_up, L0_ffn_w_down, L0_ffn_sw_gate, L0_ffn_sw_up, L0_ffn_sw_down):
    import jax
    import jax.numpy as jnp

    def _L0_xattn_ref(x, w1, w2):
        import jax, jax.numpy as jnp
        import numpy as np
        E, T, H, F = (8, 256, 128, 512)
        h = jnp.einsum('eth,efh->etf', x, w1)
        a = jax.nn.gelu(h, approximate=True)
        return jnp.einsum('etf,efh->eth', a, w2)

    def _L0_ffn_ref(hidden_states, gate_kernel, gate_bias, w_gate, w_up, w_down, sw_gate, sw_up, sw_down):
        import jax, jax.numpy as jnp
        import numpy as np
        H = 128
        M = 64
        E = 16
        TOP_K = 4
        N_GROUP = 4
        TOPK_GROUP = 2
        SCALE = 2.5
        B, S = (2, 128)

        def _gate(x2d, gate_kernel, gate_bias):
            n = x2d.shape[0]
            logits = jnp.dot(x2d.astype(jnp.float32), gate_kernel.astype(jnp.float32))
            scores = jax.nn.sigmoid(logits)
            scores_for_choice = scores + gate_bias
            group_scores = scores_for_choice.reshape(n, N_GROUP, E // N_GROUP)
            top2 = jax.lax.top_k(group_scores, k=2)[0]
            group_sum = jnp.sum(top2, axis=-1)
            group_idx = jax.lax.top_k(group_sum, k=TOPK_GROUP)[1]
            group_mask = jnp.zeros_like(group_sum).at[jnp.arange(n)[:, None], group_idx].set(1.0)
            score_mask = jnp.repeat(group_mask[:, :, None], E // N_GROUP, axis=2).reshape(n, E)
            masked_scores = jnp.where(score_mask > 0, scores_for_choice, 0.0)
            topk_weight, topk_idx = jax.lax.top_k(masked_scores, k=TOP_K)
            topk_weight = topk_weight / (jnp.sum(topk_weight, axis=-1, keepdims=True) + 1e-20)
            topk_weight = topk_weight * SCALE
            return (topk_idx, topk_weight)
        orig_shape = hidden_states.shape
        x = hidden_states.reshape(-1, orig_shape[-1])
        topk_idx, topk_weight = _gate(x, gate_kernel, gate_bias)
        onehot = (topk_idx[:, :, None] == jnp.arange(E)[None, None, :]).astype(topk_weight.dtype)
        combine = jnp.einsum('nke,nk->ne', onehot, topk_weight)
        g = jnp.einsum('nh,ehm->enm', x, w_gate)
        u = jnp.einsum('nh,ehm->enm', x, w_up)
        inter = jax.nn.silu(g) * u
        y_e = jnp.einsum('enm,emh->enh', inter, w_down)
        y = jnp.einsum('ne,enh->nh', combine, y_e)
        shared = jnp.dot(jax.nn.silu(jnp.dot(x, sw_gate)) * jnp.dot(x, sw_up), sw_down)
        return (y + shared).reshape(orig_shape)
    x = x + jnp.tanh(g_xattn[0]) * _L0_xattn_ref(_layernorm(x, axis=-1), ctx_1024, ctx_1024)
    x = x + jnp.tanh(g_ffn[0]) * _L0_ffn_ref(_layernorm(x, axis=-1), L0_ffn_gate_kernel, L0_ffn_gate_bias, L0_ffn_w_gate, L0_ffn_w_up, L0_ffn_w_down, L0_ffn_sw_gate, L0_ffn_sw_up, L0_ffn_sw_down)
    return x

_drawn_inputs = setup_inputs


def setup_inputs(seed=0):
    import zlib

    import numpy as np

    out = dict(_drawn_inputs(seed))
    spreads = {}
    factors = {}
    for name, (base, spread) in spreads.items():
        noise = np.random.default_rng([zlib.crc32(name.encode()), seed]).standard_normal(out[name].shape)
        drawn = base * np.exp(spread * noise) if base else spread * noise
        out[name] = jnp.asarray(drawn.astype(out[name].dtype))
    for name, factor in factors.items():
        out[name] = (out[name] * factor).astype(out[name].dtype)
    return out
```

```python
from contextlib import ExitStack

import concourse.bass as bass
from concourse import mybir

ALU = mybir.AluOpType
ACT = mybir.ActivationFunctionType
AX = mybir.AxisListType
F32 = mybir.dt.float32
F32R = mybir.dt.float32r

P = 128
NB = 4
S = 512
J = S // P
H = 128
C = 77
E = 16
M = 64
NG = 4
EG = E // NG
TOPG = 2
TOPK = 4
EX = E + EG
ROUTE_SCALE = 2.5
KB = 1 + E * M // P
SLOTS = NB * KB
EPS = 1e-5
BIG = 1e30
PICKED = -1e30
GELU_C = 0.7978845608028654
GELU_A = 0.044715
RING = 12


def lag(i):
    if i <= 12:
        return 8
    if i == 13:
        return 7
    if i <= 30:
        return 6
    return {31: 5, 32: 5, 33: 4, 34: 4, 35: 3}[i]


def plan_downs():
    out, done = [], 0
    for i in range(SLOTS):
        n = max(done, i + 1 - lag(i))
        out.append(list(range(done, n)))
        done = n
    out.append(list(range(done, SLOTS)))
    return out


DOWNS = plan_downs()
LAST_DOWN = [next(i for i in range(SLOTS + 1) if KB * b + KB - 1 in DOWNS[i]) for b in range(NB)]
for _b in range(NB - 1):
    assert KB * (_b + 1) not in DOWNS[LAST_DOWN[_b]]

R_OPS = [1, 2, 3, 1, 1, 2, 1, 1, 1, 1, 4, 5, 2, 1, 1]
R_ALL = sum(R_OPS)


def router_slots(b):
    n, first = (5, 0) if b == 0 else (3, KB * (b - 1) + 6)
    return {first + s: list(range(n * s, min(n * s + n, len(R_OPS)))) for s in range(-(-len(R_OPS) // n))}


R_SLOTS = [router_slots(b) for b in range(NB)]
CT_SLOT = [max(r) + 1 for r in R_SLOTS]


def flamingo_block(nc, x, ctx_in, g_xattn, g_ffn, gate_kernel, gate_bias, w_gate, w_up, w_down,
                   sw_gate, sw_up, sw_down, c_dram, out):
    with ExitStack() as es:
        def sb(name, shape, dt=F32):
            return es.enter_context(nc.sbuf_tensor(name, shape, dt))

        def bank(name):
            return es.enter_context(nc.psum_tensor(name, [P, S], F32))

        def sem(name):
            return es.enter_context(nc.semaphore(name))

        ident = sb("ident", [P, P])
        before = sb("before", [P, NG, NG])
        minus_half = sb("minus_half", [P, J])
        ctx_sb = sb("ctx_sb", [C, NB, H])
        ctxT = sb("ctxT", [P, NB, C])
        gates = sb("gates", [P, 2])
        gates_t = sb("gates_t", [P, 2])
        gx_half = sb("gx_half", [P, 1])
        bias_b = sb("bias_b", [P, E])
        bias_h = sb("bias_h", [P, E])
        gk = sb("gk", [P, E])
        gk_hi = sb("gk_hi", [P, E], F32R)
        gk_lo = sb("gk_lo", [P, E], F32R)
        w_raw = sb("w_raw", [P, KB, 3, P])
        w_hi = sb("w_hi", [P, KB, 3, P], F32R)
        w_lo = sb("w_lo", [P, KB, 3, P], F32R)

        xt = sb("xt", [P, NB, J, H])
        stats = sb("stats", [P, J, 6])
        mv = sb("mv", [P, J, 2])
        veps = sb("veps", [P, J])
        rstd = sb("rstd", [P, J])
        xn = sb("xn", [P, J, H])
        xnT = sb("xnT", [P, S])
        hsq = sb("hsq", [C, S])
        z = sb("z", [C, S])
        th = sb("th", [C, S])
        aT = sb("aT", [C, S])
        xh = sb("xh", [P, 2, S], F32R)
        xl = sb("xl", [P, 2, S], F32R)
        yT = sb("yT", [P, S])
        ot = sb("ot", [P, 2, J, H])

        rth = sb("rth", [P, J * E])
        sfc = sb("sfc", [P, J, EX])
        pmax = sb("pmax", [P, J * EX // 2])
        pmin = sb("pmin", [P, J * EX // 2])
        top = sb("top", [P, J * (NG + 1)])
        sec_a = sb("sec_a", [P, J * (NG + 1)])
        sec_b = sb("sec_b", [P, J * (NG + 1)])
        sec = sb("sec", [P, J * (NG + 1)])
        gs = sb("gs", [P, J, NG + 1])
        gt = sb("gt", [P, J, NG, NG])
        eq = sb("eq", [P, J, NG, NG])
        rank = sb("rank", [P, J, NG + 1])
        masked = sb("masked", [P, J, EX])
        top8 = sb("top8", [P, J, 8])
        rep = sb("rep", [P, J, EX])
        num = sb("num", [P, J, E])
        den = sb("den", [P, J])
        den2 = sb("den2", [P, J])
        rec = sb("rec", [P, J])
        comb = sb("comb", [P, J, E])
        combT = sb("combT", [E, S])
        cb = sb("cb", [P, 2, KB - 1, S])

        sg = sb("sg", [P, 3, S])
        act = sb("act", [P, RING, S])
        ah = sb("ah", [P, 2, S], F32R)
        al = sb("al", [P, 2, S], F32R)

        bank_g = [bank("bank_g0"), bank("bank_g1")]
        bank_u = [bank("bank_u0"), bank("bank_u1")]
        bank_t = bank("bank_t")
        bank_h = bank("bank_h")
        bank_l = bank("bank_l")
        bank_y = bank("bank_y")

        x_in = [sem(f"x_in{b}") for b in range(NB)]
        ctx_in_s, small_in = sem("ctx_in"), sem("small_in")
        w_in = [sem(f"w_in{n}") for n in range(3)]
        zeroed, const_ready, sentinels = sem("zeroed"), sem("const_ready"), sem("sentinels")
        gates_tanh, gates_ready, bias_ready = sem("gates_tanh"), sem("gates_ready"), sem("bias_ready")
        gk_hi_ready, gk_lo_ready = sem("gk_hi_ready"), sem("gk_lo_ready")
        w_hi_ready, w_lo_ready = sem("w_hi_ready"), sem("w_lo_ready")
        ctxT_done, ctxT_ready = sem("ctxT_done"), sem("ctxT_ready")
        stats_done, mv_ready, veps_ready, rstd_ready = sem("stats_done"), sem("mv_ready"), sem("veps_ready"), sem("rstd_ready")
        xn_ready, xnT_done, xnT_ready = sem("xn_ready"), sem("xnT_done"), sem("xnT_ready")
        xh_ready, xl_ready = sem("xh_ready"), sem("xl_ready")
        h_done, hsq_ready, z_ready, th_ready, aT_ready = sem("h_done"), sem("hsq_ready"), sem("z_ready"), sem("th_ready"), sem("aT_ready")
        attn_done, x2_ready = sem("attn_done"), sem("x2_ready")
        logits_done, rth_ready, r_step = sem("logits_done"), sem("rth_ready"), sem("r_step")
        combT_done, combT_ready, comb_out, cb_in = sem("combT_done"), sem("combT_ready"), sem("comb_out"), [sem("cb_in0"), sem("cb_in1")]
        g_done, u_done, sg_ready, act_ready, act_scaled = sem("g_done"), sem("u_done"), sem("sg_ready"), sem("act_ready"), sem("act_scaled")
        ah_ready, al_ready, down_done = sem("ah_ready"), sem("al_ready"), sem("down_done")
        y_ready, yT_done, ot_ready, out_done = sem("y_ready"), sem("yT_done"), sem("ot_ready"), sem("out_done")

        def w_chunk(k):
            return 0 if k == 0 else 1 if k <= 4 else 2

        def scaled_before(d):
            return d + 1 - (d // KB + 1)

        x_v = x.rearrange("b (p j) h -> b p j h", j=J)
        out_v = out.rearrange("b (p j) h -> b p j h", j=J)

        block = es.enter_context(nc.Block())

        @block.sync
        def _(sp):
            sp.dma_start(xt[:, 0], x_v[0]).then_inc(x_in[0], 16)
            for i, w in enumerate((sw_gate, sw_up, sw_down)):
                sp.dma_start(w_raw[:, 0, i, :], w).then_inc(w_in[0], 16)
            sp.dma_start(xt[:, 1], x_v[1]).then_inc(x_in[1], 16)
            for n, (k0, k1) in enumerate(((1, 5), (5, 9))):
                e0, e1 = 2 * (k0 - 1), 2 * (k1 - 1)
                for i, w in enumerate((w_gate, w_up)):
                    for half in range(2):
                        sp.dma_start(w_raw[:, k0:k1, i, M * half:M * half + M],
                                     w[e0:e1].rearrange("(k s) h m -> s h k m", s=2)[half]).then_inc(w_in[1 + n], 16)
                sp.dma_start(w_raw[:, k0:k1, 2, :],
                             w_down[e0:e1].rearrange("(k s) m h -> (s m) k h", s=2)).then_inc(w_in[1 + n], 16)
                sp.dma_start(xt[:, 2 + n], x_v[2 + n]).then_inc(x_in[2 + n], 16)

            def combine_round(b):
                sp.wait_ge(combT_ready, b + 1)
                sp.dma_start(c_dram[b], combT[:]).then_inc(comb_out, 16)
                sp.wait_ge(comb_out, 16 * (b + 1))
                if b >= 2:
                    sp.wait_ge(act_scaled, scaled_before(KB * (b - 1) - 1))
                for half in range(2):
                    src = c_dram[b].rearrange("(k s) t -> s k t", s=2)[half:half + 1]
                    sp.dma_start(cb[M * half:M * half + M, b % 2], src.broadcast_to([M, KB - 1, S])).then_inc(cb_in[b % 2], 16)

            def store(b):
                sp.wait_ge(ot_ready, b + 1)
                sp.dma_start(out_v[b], ot[:, b % 2]).then_inc(out_done, 16)

            combine_round(0)
            combine_round(1)
            store(0)
            combine_round(2)
            store(1)
            combine_round(3)
            store(2)
            store(3)
            sp.wait_ge(out_done, 16 * NB)
            sp.wait_ge(comb_out, 16 * NB)

        @block.gpsimd
        def _(pool):
            pool.memset(ident[:], 0.0).then_inc(zeroed, 1)
            pool.memset(before[:], 1.0).then_inc(zeroed, 1)
            pool.memset(minus_half[:], -0.5).then_inc(const_ready, 1)
            pool.wait_ge(zeroed, 2)
            pool.affine_select(out=ident[:], in_=ident[:], compare_op=ALU.not_equal, fill=1.0, base=0,
                               pattern=[[-1, P]], channel_multiplier=1).then_inc(const_ready, 1)
            pool.affine_select(out=before[:], in_=before[:], compare_op=ALU.is_gt, fill=0.0, base=0,
                               pattern=[[1, NG], [-1, NG]], channel_multiplier=0).then_inc(const_ready, 1)

            def inv_std(n):
                pool.wait_ge(mv_ready, J * (n + 1))
                if n:
                    pool.wait_ge(rstd_ready, n)
                pool.tensor_scalar(veps[:], mv[:, :, 1], EPS, None, ALU.add).then_inc(veps_ready, 1)
                pool.wait_ge(veps_ready, n + 1)
                if n:
                    pool.wait_ge(xn_ready, J * n)
                pool.tensor_tensor(rstd[:], veps[:], minus_half[:], ALU.pow).then_inc(rstd_ready, 1)

            def split_lo(k):
                pool.wait_ge(w_hi_ready, k + 1)
                pool.tensor_tensor(w_lo[:, k], w_raw[:, k], w_hi[:, k].bitcast(F32), ALU.subtract).then_inc(w_lo_ready, 1)

            def scale(d):
                b, k = divmod(d, KB)
                if k == 0:
                    return
                if k == 1:
                    pool.wait_ge(cb_in[b % 2], 32 * (b // 2 + 1))
                pool.wait_ge(act_ready, d + 1)
                pool.tensor_tensor(act[:, d % RING], act[:, d % RING], cb[:, b % 2, k - 1], ALU.mult).then_inc(act_scaled, 1)

            pool.wait_ge(const_ready, 3)
            inv_std(0)
            pool.wait_ge(gk_hi_ready, 1)
            pool.tensor_tensor(gk_lo[:], gk[:], gk_hi[:].bitcast(F32), ALU.subtract).then_inc(gk_lo_ready, 1)
            split_lo(0)
            split_lo(1)
            inv_std(1)
            split_lo(2)
            inv_std(2)
            for k in range(3, KB):
                split_lo(k)
            scaled = 0
            for i in range(SLOTS):
                b, k = divmod(i, KB)
                if k == 4 and b + 1 < NB:
                    inv_std(2 * b + 3)
                if k == 7 and b + 2 < NB:
                    inv_std(2 * b + 4)
                ahead = max(DOWNS[min(i + 2, SLOTS)], default=-1) + 1
                while scaled < ahead:
                    scale(scaled)
                    scaled += 1
            while scaled < SLOTS:
                scale(scaled)
                scaled += 1

        @block.scalar
        def _(act_e):
            act_e.dma_start(gates[:, 0:1], g_xattn.partition_broadcast(P)).then_inc(small_in, 16)
            act_e.dma_start(gates[:, 1:2], g_ffn.partition_broadcast(P)).then_inc(small_in, 16)
            act_e.dma_start(bias_b[:], gate_bias.partition_broadcast(P)).then_inc(small_in, 16)
            act_e.dma_start(gk[:], gate_kernel).then_inc(small_in, 16)
            act_e.dma_start(ctx_sb[:], ctx_in.rearrange("b c h -> c b h")).then_inc(ctx_in_s, 16)
            act_e.wait_ge(small_in, 64)
            act_e.activation(gates_t[:], gates[:], ACT.Tanh).then_inc(gates_tanh, 1)
            act_e.activation(gk_hi[:], gk[:], ACT.Copy).then_inc(gk_hi_ready, 1)
            act_e.wait_ge(ctxT_done, 1)
            act_e.activation(ctxT[:], bank_l[:, 0:NB * C].rearrange("p (b c) -> p b c", b=NB), ACT.Copy).then_inc(ctxT_ready, 1)

            def split_hi(k):
                c = w_chunk(k)
                act_e.wait_ge(w_in[c], 48 if c == 0 else 80)
                act_e.activation(w_hi[:, k], w_raw[:, k], ACT.Copy).then_inc(w_hi_ready, 1)

            def evac_xnT(b):
                act_e.wait_ge(xnT_done, 2 * b + 1)
                if b:
                    act_e.wait_ge(h_done, b)
                act_e.activation(xnT[:], bank_t[:], ACT.Copy).then_inc(xnT_ready, 1)

            def square_h(b):
                act_e.wait_ge(h_done, b + 1)
                if b:
                    act_e.wait_ge(z_ready, b)
                act_e.activation(hsq[:], bank_h[0:C], ACT.Square).then_inc(hsq_ready, 1)

            def tanh_z(b):
                act_e.wait_ge(z_ready, b + 1)
                if b:
                    act_e.wait_ge(aT_ready, b)
                act_e.activation(th[:], z[:], ACT.Tanh, scale=GELU_C * GELU_A).then_inc(th_ready, 1)

            def split_x_hi(b):
                act_e.wait_ge(xnT_done, 2 * b + 2)
                if b >= 2:
                    act_e.wait_ge(u_done, KB * (b - 1))
                    act_e.wait_ge(logits_done, b - 1)
                act_e.activation(xh[:, b % 2], bank_t[:], ACT.Copy).then_inc(xh_ready, 1)

            def tanh_logits(b):
                act_e.wait_ge(logits_done, b + 1)
                if b:
                    act_e.wait_ge(r_step, R_ALL * (b - 1) + 1)
                act_e.activation(rth[:], bank_l[:, 0:J * E], ACT.Tanh, scale=0.5).then_inc(rth_ready, 1)

            def evac_combT(b):
                act_e.wait_ge(combT_done, b + 1)
                if b:
                    act_e.wait_ge(comb_out, 16 * b)
                act_e.activation(combT[:], bank_l[0:E], ACT.Copy).then_inc(combT_ready, 1)

            def silu(i):
                act_e.wait_ge(g_done, i + 1)
                if i >= 3:
                    act_e.wait_ge(act_ready, i - 2)
                act_e.activation(sg[:, i % 3], bank_g[i % 2][:], ACT.Silu).then_inc(sg_ready, 1)

            def split_act_hi(d):
                if d % KB:
                    act_e.wait_ge(act_scaled, scaled_before(d))
                else:
                    act_e.wait_ge(act_ready, d + 1)
                if d >= 2:
                    act_e.wait_ge(down_done, d - 1)
                act_e.activation(ah[:, d % 2], act[:, d % RING], ACT.Copy).then_inc(ah_ready, 1)

            def evac_y(b):
                act_e.wait_ge(down_done, KB * (b + 1))
                if b:
                    act_e.wait_ge(yT_done, b)
                act_e.activation(yT[:], bank_y[:], ACT.Copy, scale=gates_t[:, 1:2]).then_inc(y_ready, 1)

            evac_xnT(0)
            split_hi(0)
            square_h(0)
            tanh_z(0)
            split_hi(1)
            split_hi(2)
            split_x_hi(0)
            tanh_logits(0)
            for k in range(3, KB):
                split_hi(k)
            for i in range(SLOTS + 1):
                b, k = divmod(i, KB)
                for n in range(NB):
                    if i == LAST_DOWN[n] + 1:
                        evac_y(n)
                    if i == CT_SLOT[n]:
                        evac_combT(n)
                if b + 1 < NB:
                    if k == 0:
                        evac_xnT(b + 1)
                    if k == 1:
                        square_h(b + 1)
                    if k == 2:
                        tanh_z(b + 1)
                    if k == 5:
                        split_x_hi(b + 1)
                    if k == 6:
                        tanh_logits(b + 1)
                if i < SLOTS:
                    silu(i)
                    for d in DOWNS[i + 1]:
                        split_act_hi(d)
            evac_y(NB - 1)

        @block.vector
        def _(dve):
            def layer_stats(n):
                b = n // 2
                if n % 2 == 0:
                    dve.wait_ge(x_in[b], 16)
                else:
                    dve.wait_ge(x2_ready, b + 1)
                for j in range(J):
                    dve.bn_stats(stats[:, j], xt[:, b, j]).then_inc(stats_done, 1)
                if n:
                    dve.wait_ge(veps_ready, n)
                for j in range(J):
                    dve.wait_ge(stats_done, J * n + j + 1)
                    dve.bn_aggr(mv[:, j], stats[:, j]).then_inc(mv_ready, 1)

            def normalise(n):
                dve.wait_ge(rstd_ready, n + 1)
                dve.wait_ge(mv_ready, J * (n + 1))
                if n:
                    dve.wait_ge(xnT_done, n)
                for j in range(J):
                    dve.tensor_scalar(xn[:, j], xt[:, n // 2, j], mv[:, j, 0:1], rstd[:, j:j + 1],
                                      ALU.subtract, ALU.mult).then_inc(xn_ready, 1)

            def gelu_z(b):
                dve.wait_ge(hsq_ready, b + 1)
                if b:
                    dve.wait_ge(th_ready, b)
                dve.scalar_tensor_tensor(z[:], hsq[:], 1.0 / GELU_A, bank_h[0:C], ALU.add, ALU.mult).then_inc(z_ready, 1)

            def gelu_a(b):
                dve.wait_ge(th_ready, b + 1)
                if b:
                    dve.wait_ge(attn_done, b)
                dve.scalar_tensor_tensor(aT[:], th[:], 1.0, bank_h[0:C], ALU.add, ALU.mult).then_inc(aT_ready, 1)

            def residual(b):
                dve.wait_ge(attn_done, b + 1)
                dve.wait_ge(gates_ready, 1)
                dve.scalar_tensor_tensor(xt[:, b], bank_h[:].rearrange("p (j h) -> p j h", j=J), gx_half[:, 0:1], xt[:, b],
                                         ALU.mult, ALU.add).then_inc(x2_ready, 1)

            def split_x_lo(b):
                dve.wait_ge(xh_ready, b + 1)
                dve.tensor_tensor(xl[:, b % 2], bank_t[:], xh[:, b % 2].bitcast(F32), ALU.subtract).then_inc(xl_ready, 1)

            def router(b, n):
                done = R_ALL * b + sum(R_OPS[:n])
                if done:
                    dve.wait_ge(r_step, done)
                masked_v = masked[:].rearrange("p j e -> p (j e)").rearrange("p (g e) -> p g e", e=EG)
                sfc_v = sfc[:].rearrange("p j e -> p (j e)").rearrange("p (g e) -> p g e", e=EG)
                pairs = sfc[:].rearrange("p j e -> p (j e)").rearrange("p (q r) -> p r q", r=2)
                if n == 0:
                    dve.wait_ge(rth_ready, b + 1)
                    dve.scalar_tensor_tensor(sfc[:, :, 0:E], rth[:].rearrange("p (j e) -> p j e", j=J), 0.5,
                                             bias_h[:].unsqueeze(1).broadcast_to([P, J, E]), ALU.mult, ALU.add).then_inc(r_step, 1)
                elif n == 1:
                    dve.tensor_tensor(pmax[:], pairs[:, 0], pairs[:, 1], ALU.max).then_inc(r_step, 1)
                    dve.tensor_tensor(pmin[:], pairs[:, 0], pairs[:, 1], ALU.min).then_inc(r_step, 1)
                elif n == 2:
                    mx = pmax[:].rearrange("p (q r) -> p r q", r=2)
                    mn = pmin[:].rearrange("p (q r) -> p r q", r=2)
                    dve.tensor_tensor(top[:], mx[:, 0], mx[:, 1], ALU.max).then_inc(r_step, 1)
                    dve.tensor_tensor(sec_a[:], mx[:, 0], mx[:, 1], ALU.min).then_inc(r_step, 1)
                    dve.tensor_tensor(sec_b[:], mn[:, 0], mn[:, 1], ALU.max).then_inc(r_step, 1)
                elif n == 3:
                    dve.tensor_tensor(sec[:], sec_a[:], sec_b[:], ALU.max).then_inc(r_step, 1)
                elif n == 4:
                    dve.tensor_tensor(gs[:].rearrange("p j g -> p (j g)"), top[:], sec[:], ALU.add).then_inc(r_step, 1)
                elif n == 5:
                    other = gs[:, :, 0:NG].unsqueeze(2).broadcast_to([P, J, NG, NG])
                    own = gs[:, :, 0:NG].unsqueeze(3).broadcast_to([P, J, NG, NG])
                    dve.tensor_tensor(gt[:], other, own, ALU.is_gt).then_inc(r_step, 1)
                    dve.tensor_tensor(eq[:], other, own, ALU.is_equal).then_inc(r_step, 1)
                elif n == 6:
                    dve.tensor_tensor(eq[:], eq[:], before[:].unsqueeze(1).broadcast_to([P, J, NG, NG]), ALU.mult).then_inc(r_step, 1)
                elif n == 7:
                    dve.tensor_tensor(gt[:], gt[:], eq[:], ALU.add).then_inc(r_step, 1)
                elif n == 8:
                    dve.tensor_reduce(rank[:, :, 0:NG], gt[:], AX.X, ALU.add).then_inc(r_step, 1)
                elif n == 9:
                    dve.scalar_tensor_tensor(masked_v, rank[:].rearrange("p j g -> p (j g)").unsqueeze(2).broadcast_to([P, J * (NG + 1), EG]),
                                             float(TOPG), sfc_v, ALU.is_lt, ALU.mult).then_inc(r_step, 1)
                elif n == 10:
                    for j in range(J):
                        dve.max(top8[:, j], masked[:, j]).then_inc(r_step, 1)
                elif n == 11:
                    for j in range(J):
                        dve.match_replace(rep[:, j], top8[:, j], masked[:, j], PICKED).then_inc(r_step, 1)
                    dve.tensor_reduce(den[:], top8[:, :, EG:8], AX.X, ALU.add).then_inc(r_step, 1)
                elif n == 12:
                    dve.tensor_scalar(den2[:], den[:], 1e-20, 1.0 / ROUTE_SCALE, ALU.add, ALU.mult).then_inc(r_step, 1)
                    dve.scalar_tensor_tensor(num[:], rep[:, :, 0:E], PICKED, masked[:, :, 0:E], ALU.is_equal, ALU.mult).then_inc(r_step, 1)
                elif n == 13:
                    dve.reciprocal(rec[:], den2[:]).then_inc(r_step, 1)
                elif n == 14:
                    if b:
                        dve.wait_ge(combT_done, b)
                    dve.tensor_tensor(comb[:], num[:], rec[:].unsqueeze(2).broadcast_to([P, J, E]), ALU.mult).then_inc(r_step, 1)

            def gate_up(i):
                dve.wait_ge(sg_ready, i + 1)
                dve.wait_ge(u_done, i + 1)
                if i >= RING:
                    dve.wait_ge(al_ready, i - RING + 1)
                dve.tensor_tensor(act[:, i % RING], sg[:, i % 3], bank_u[i % 2][:], ALU.mult).then_inc(act_ready, 1)

            def split_act_lo(d):
                dve.wait_ge(ah_ready, d + 1)
                dve.tensor_tensor(al[:, d % 2], act[:, d % RING], ah[:, d % 2].bitcast(F32), ALU.subtract).then_inc(al_ready, 1)

            def finish(b):
                dve.wait_ge(yT_done, b + 1)
                if b >= 2:
                    dve.wait_ge(out_done, 16 * (b - 1))
                dve.tensor_tensor(ot[:, b % 2], bank_h[:].rearrange("p (j h) -> p j h", j=J), xt[:, b], ALU.add).then_inc(ot_ready, 1)

            dve.memset(sfc[:], BIG).then_inc(sentinels, 1)
            dve.memset(rank[:], 0.0).then_inc(sentinels, 1)
            layer_stats(0)
            dve.wait_ge(gates_tanh, 1)
            dve.tensor_scalar(gx_half[:], gates_t[:, 0:1], 0.5, None, ALU.mult).then_inc(gates_ready, 1)
            dve.tensor_scalar(bias_h[:], bias_b[:], 0.5, None, ALU.add).then_inc(bias_ready, 1)
            normalise(0)
            gelu_z(0)
            gelu_a(0)
            residual(0)
            layer_stats(1)
            normalise(1)
            layer_stats(2)
            split_x_lo(0)
            normalise(2)
            dve.wait_ge(sentinels, 2)
            dve.wait_ge(bias_ready, 1)
            for i in range(SLOTS + 1):
                b, k = divmod(i, KB)
                for n in range(NB):
                    if i == LAST_DOWN[n] + 2:
                        finish(n)
                steps = [(n, s) for n in range(NB) for s in R_SLOTS[n].get(i, [])]
                if steps:
                    router(*steps[0])
                if i < SLOTS:
                    gate_up(i)
                if len(steps) > 1:
                    router(*steps[1])
                if i < SLOTS:
                    for d in DOWNS[i + 1]:
                        split_act_lo(d)
                for s in steps[2:]:
                    router(*s)
                if b + 1 < NB:
                    if k == 1:
                        gelu_z(b + 1)
                    if k == 2:
                        gelu_a(b + 1)
                    if k == 3:
                        residual(b + 1)
                        layer_stats(2 * b + 3)
                    if k == 4:
                        normalise(2 * b + 3)
                    if k == 5:
                        split_x_lo(b + 1)
                if b + 2 < NB:
                    if k == 6:
                        layer_stats(2 * b + 4)
                    if k == 8:
                        normalise(2 * b + 4)
            finish(NB - 1)

        @block.tensor
        def _(pe):
            h_readers = []

            def bank_h_free():
                if h_readers:
                    s, v = h_readers[-1]
                    pe.wait_ge(s, v)

            def transpose_xn(n):
                pe.wait_ge(xn_ready, J * (n + 1))
                b = n // 2
                if n % 2:
                    pe.wait_ge(xnT_ready, b + 1)
                elif n:
                    pe.wait_ge(xl_ready, b)
                for j in range(J):
                    last = pe.transpose(bank_t[:, j * P:(j + 1) * P], xn[:, j], ident[:])
                last.then_inc(xnT_done, 1)

            def hidden(b):
                pe.wait_ge(xnT_ready, b + 1)
                bank_h_free()
                pe.matmul(bank_h[0:C], ctxT[:, b], xnT[:], start=True, stop=True).then_inc(h_done, 1)
                h_readers.append((aT_ready, b + 1))

            def attend(b):
                pe.wait_ge(aT_ready, b + 1)
                for j in range(J):
                    last = pe.matmul(bank_h[:, j * H:(j + 1) * H], aT[:, j * P:(j + 1) * P], ctx_sb[:, b], start=True, stop=True)
                last.then_inc(attn_done, 1)
                h_readers.append((x2_ready, b + 1))

            def logits(b):
                pe.wait_ge(xl_ready, b + 1)
                if b:
                    pe.wait_ge(combT_ready, b)
                for j in range(J):
                    o = bank_l[:, j * E:(j + 1) * E]
                    t = slice(j * P, (j + 1) * P)
                    pe.matmul(o, xh[:, b % 2, t], gk_hi[:], start=True, stop=False)
                    pe.matmul(o, xh[:, b % 2, t], gk_lo[:], start=False, stop=False)
                    last = pe.matmul(o, xl[:, b % 2, t], gk_hi[:], start=False, stop=True)
                last.then_inc(logits_done, 1)

            def transpose_comb(b):
                pe.wait_ge(r_step, R_ALL * (b + 1))
                pe.wait_ge(rth_ready, b + 1)
                for j in range(J):
                    last = pe.transpose(bank_l[0:E, j * P:(j + 1) * P], comb[:, j], ident[:])
                last.then_inc(combT_done, 1)

            def three(o, k, i, hi, lo, start, stop):
                pe.matmul(o, w_lo[:, k, i], hi, start=start, stop=False)
                pe.matmul(o, w_hi[:, k, i], hi, start=False, stop=False)
                return pe.matmul(o, w_hi[:, k, i], lo, start=False, stop=stop)

            def gate_up(i):
                b, k = divmod(i, KB)
                if k == 0:
                    pe.wait_ge(xl_ready, b + 1)
                if b == 0:
                    pe.wait_ge(w_lo_ready, k + 1)
                if i >= 2:
                    pe.wait_ge(act_ready, i - 1)
                hi, lo = xh[:, b % 2], xl[:, b % 2]
                three(bank_g[i % 2][:], k, 0, hi, lo, True, True).then_inc(g_done, 1)
                three(bank_u[i % 2][:], k, 1, hi, lo, True, True).then_inc(u_done, 1)

            def down(d):
                b, k = divmod(d, KB)
                pe.wait_ge(al_ready, d + 1)
                if k == 0 and b:
                    pe.wait_ge(y_ready, b)
                three(bank_y[:], k, 2, ah[:, d % 2], al[:, d % 2], k == 0, k == KB - 1).then_inc(down_done, 1)

            def transpose_y(b):
                pe.wait_ge(y_ready, b + 1)
                bank_h_free()
                for j in range(J):
                    last = pe.transpose(bank_h[:, j * H:(j + 1) * H], yT[:, j * P:(j + 1) * P], ident[:])
                last.then_inc(yT_done, 1)
                h_readers.append((ot_ready, b + 1))

            pe.wait_ge(const_ready, 3)
            pe.wait_ge(ctx_in_s, 16)
            for b in range(NB):
                last = pe.transpose(bank_l[:, b * C:(b + 1) * C], ctx_sb[:, b], ident[0:C, 0:C])
            last.then_inc(ctxT_done, 1)
            transpose_xn(0)
            pe.wait_ge(ctxT_ready, 1)
            hidden(0)
            attend(0)
            transpose_xn(1)
            pe.wait_ge(gk_lo_ready, 1)
            logits(0)
            for i in range(SLOTS + 1):
                b, k = divmod(i, KB)
                if b + 1 < NB:
                    if k == 0:
                        transpose_xn(2 * b + 2)
                    if k == 1:
                        hidden(b + 1)
                    if k == 3:
                        attend(b + 1)
                    if k == 5:
                        transpose_xn(2 * b + 3)
                    if k == 6:
                        logits(b + 1)
                for n in range(NB):
                    if i == CT_SLOT[n]:
                        transpose_comb(n)
                    if i == LAST_DOWN[n] + 2:
                        transpose_y(n)
                if i < SLOTS:
                    gate_up(i)
                for d in DOWNS[i]:
                    down(d)
            transpose_y(NB - 1)


_INS = ['x', 'ctx_1024', 'g_xattn', 'g_ffn', 'L0_ffn_gate_kernel', 'L0_ffn_gate_bias', 'L0_ffn_w_gate', 'L0_ffn_w_up',
        'L0_ffn_w_down', 'L0_ffn_sw_gate', 'L0_ffn_sw_up', 'L0_ffn_sw_down']


def kernel(**inputs):
    import numpy as _np
    import concourse.bacc as _bacc
    from concourse import mybir as _mybir
    from concourse.bass_utils import run_bass_kernel_spmd as _run

    nc = _bacc.Bacc("TRN2", target_bir_lowering=False, num_devices=1)
    arrays, args = {}, []
    for name in _INS:
        a = _np.ascontiguousarray(inputs[name])
        arrays[f"in_{name}_dram"] = a
        args.append(nc.dram_tensor(f"in_{name}_dram", a.shape, _mybir.dt.from_np(a.dtype), kind="ExternalInput").ap())
    args.append(nc.dram_tensor("combine_weights", (NB, E, S), F32, kind="Internal").ap())
    args.append(nc.dram_tensor("out_0_dram", (NB, S, H), F32, kind="ExternalOutput").ap())
    flamingo_block(nc, *args)
    r = _run(nc, [arrays], core_ids=[0])
    return r.results[0]["out_0_dram"]
```

```python
from contextlib import ExitStack

import concourse.bass as bass
from concourse import mybir

ALU = mybir.AluOpType
ACT = mybir.ActivationFunctionType
AX = mybir.AxisListType
F32 = mybir.dt.float32
F32R = mybir.dt.float32r

P = 128
NB = 4
S = 512
J = S // P
H = 128
C = 77
E = 16
M = 64
NG = 4
EG = E // NG
TOPG = 2
TOPK = 4
EX = E + EG
ROUTE_SCALE = 2.5
KB = 1 + E * M // P
SLOTS = NB * KB
EPS = 1e-5
BIG = 1e30
PICKED = -1e30
GELU_C = 0.7978845608028654
GELU_A = 0.044715
RING = 12


def lag(i):
    if i <= 12:
        return 8
    if i == 13:
        return 7
    if i <= 30:
        return 6
    return {31: 5, 32: 5, 33: 4, 34: 4, 35: 3}[i]


def plan_downs():
    out, done = [], 0
    for i in range(SLOTS):
        n = max(done, i + 1 - lag(i))
        out.append(list(range(done, n)))
        done = n
    out.append(list(range(done, SLOTS)))
    return out


DOWNS = plan_downs()
LAST_DOWN = [next(i for i in range(SLOTS + 1) if KB * b + KB - 1 in DOWNS[i]) for b in range(NB)]
for _b in range(NB - 1):
    assert KB * (_b + 1) not in DOWNS[LAST_DOWN[_b]]

BASE = [-8] + [max(-3, KB * b - 13) for b in range(1, NB)]
R_STATS1, R_RSTD1, R_NORM1 = -4, -3, -2
R_T1, R_HIDDEN, R_GELU, R_ATTEND = 0, 1, 2, 4
R_RSTD2, R_NORM2, R_T2, R_LOGITS = 5, 6, 7, 8
FIRST = BASE[0] + R_STATS1

R_OPS = [0, 1, 2, 3, 1, 1, 2, 1, 1, 1, 1, 4, 5, 2, 1, 1]
R_ALL = sum(R_OPS)


def router_slots(b):
    out, at = {BASE[b] + R_LOGITS: [0]}, 1
    slot = BASE[b] + R_LOGITS + 1
    while at < len(R_OPS):
        n = 5 if b == 0 else 3
        out[slot] = list(range(at, min(at + n, len(R_OPS))))
        at, slot = at + n, slot + 1
    return out


R_SLOTS = [router_slots(b) for b in range(NB)]
CT_SLOT = [max(r) + 1 for r in R_SLOTS]
Y_SLOT = [s + 1 for s in LAST_DOWN]
YT_SLOT = [s + 2 for s in LAST_DOWN]
LAST = SLOTS + 3
W_SPLIT = {-9: 1, -7: 1, -5: 1, -3: 2, -2: 1, -1: 1, 0: 1, 1: 1}
assert sum(W_SPLIT.values()) == KB


def flamingo_block(nc, x, ctx_in, g_xattn, g_ffn, gate_kernel, gate_bias, w_gate, w_up, w_down,
                   sw_gate, sw_up, sw_down, c_dram, out):
    with ExitStack() as es:
        def sb(name, shape, dt=F32):
            return es.enter_context(nc.sbuf_tensor(name, shape, dt))

        def bank(name):
            return es.enter_context(nc.psum_tensor(name, [P, S], F32))

        def sem(name):
            return es.enter_context(nc.semaphore(name))

        ident = sb("ident", [P, P])
        before = sb("before", [P, NG, NG])
        minus_half = sb("minus_half", [P, J])
        warm = sb("warm", [P, 1])
        ctx_sb = sb("ctx_sb", [C, NB, H])
        ctxT = sb("ctxT", [P, NB, C])
        gates = sb("gates", [P, 2])
        gates_t = sb("gates_t", [P, 2])
        gx_half = sb("gx_half", [P, 1])
        bias_b = sb("bias_b", [P, E])
        bias_h = sb("bias_h", [P, E])
        gk = sb("gk", [P, E])
        gk_parts = sb("gk_parts", [P, 2, E], F32R)
        w_raw = sb("w_raw", [P, KB, 3, P])
        w_hi = sb("w_hi", [P, KB, 3, P], F32R)
        w_lo = sb("w_lo", [P, KB, 3, P], F32R)

        xt = sb("xt", [P, NB, J, H])
        stats = sb("stats", [P, J, 6])
        mv = sb("mv", [P, 2, J, 2])
        veps = sb("veps", [P, J])
        rstd = sb("rstd", [P, 2, J])
        xn = sb("xn", [P, 2, J, H])
        xnT = sb("xnT", [P, S])
        hsq = sb("hsq", [C, S])
        z = sb("z", [C, S])
        th = sb("th", [C, S])
        aT = sb("aT", [C, S])
        xh = sb("xh", [P, 2, S], F32R)
        xl = sb("xl", [P, 2, S], F32R)
        yT = sb("yT", [P, S])
        ot = sb("ot", [P, 2, J, H])

        lg = sb("lg", [P, J * E])
        rth = sb("rth", [P, J * E])
        sfc = sb("sfc", [P, J, EX])
        pmax = sb("pmax", [P, J * EX // 2])
        pmin = sb("pmin", [P, J * EX // 2])
        top = sb("top", [P, J * (NG + 1)])
        sec_a = sb("sec_a", [P, J * (NG + 1)])
        sec_b = sb("sec_b", [P, J * (NG + 1)])
        sec = sb("sec", [P, J * (NG + 1)])
        gs = sb("gs", [P, J, NG + 1])
        gt = sb("gt", [P, J, NG, NG])
        eq = sb("eq", [P, J, NG, NG])
        rank = sb("rank", [P, J, NG + 1])
        masked = sb("masked", [P, J, EX])
        top8 = sb("top8", [P, J, 8])
        rep = sb("rep", [P, J, EX])
        num = sb("num", [P, J, E])
        den = sb("den", [P, J])
        den2 = sb("den2", [P, J])
        rec = sb("rec", [P, J])
        comb = sb("comb", [P, E, J])
        combT = sb("combT", [E * J, P])
        cb = sb("cb", [P, 2, KB - 1, S])

        sg = sb("sg", [P, 3, S])
        act = sb("act", [P, RING, S])
        ah = sb("ah", [P, 2, S], F32R)
        al = sb("al", [P, 2, S], F32R)

        bank_g = [bank("bank_g0"), bank("bank_g1")]
        bank_u = [bank("bank_u0"), bank("bank_u1")]
        bank_t = bank("bank_t")
        bank_h = bank("bank_h")
        bank_l = bank("bank_l")
        bank_y = bank("bank_y")

        x_in = [sem(f"x_in{b}") for b in range(NB)]
        ctx_in_s, small_in = sem("ctx_in"), sem("small_in")
        w_in = [sem(f"w_in{n}") for n in range(3)]
        zeroed, const_ready, sentinels = sem("zeroed"), sem("const_ready"), sem("sentinels")
        gates_tanh, gates_ready, bias_ready = sem("gates_tanh"), sem("gates_ready"), sem("bias_ready")
        gk_hi_ready, gk_lo_ready = sem("gk_hi_ready"), sem("gk_lo_ready")
        w_hi_ready, w_lo_ready = sem("w_hi_ready"), sem("w_lo_ready")
        ctxT_done, ctxT_ready = sem("ctxT_done"), sem("ctxT_ready")
        stats_done, mv_ready = sem("stats_done"), [sem("mv1_ready"), sem("mv2_ready")]
        veps_ready, rstd_ready = sem("veps_ready"), [sem("rstd1_ready"), sem("rstd2_ready")]
        xn_ready, xnT_done = [sem("xn1_ready"), sem("xn2_ready")], [sem("xn1T_done"), sem("xn2T_done")]
        xnT_ready = sem("xnT_ready")
        lg_ready = sem("lg_ready")
        warm_ready, silu_warm = sem("warm_ready"), sem("silu_warm")
        xh_ready, xl_ready = sem("xh_ready"), sem("xl_ready")
        h_done, hsq_ready, z_ready, th_ready, aT_ready = sem("h_done"), sem("hsq_ready"), sem("z_ready"), sem("th_ready"), sem("aT_ready")
        attn_done, x2_ready = sem("attn_done"), sem("x2_ready")
        logits_done, rth_ready, r_step = sem("logits_done"), sem("rth_ready"), sem("r_step")
        combT_done, combT_ready, comb_out, cb_in = sem("combT_done"), sem("combT_ready"), sem("comb_out"), [sem("cb_in0"), sem("cb_in1")]
        g_done, u_done, sg_ready, act_ready, act_scaled = sem("g_done"), sem("u_done"), sem("sg_ready"), sem("act_ready"), sem("act_scaled")
        ah_ready, al_ready, down_done = sem("ah_ready"), sem("al_ready"), sem("down_done")
        y_ready, yT_done, ot_ready, out_done = sem("y_ready"), sem("yT_done"), sem("ot_ready"), sem("out_done")

        def w_chunk(k):
            return 0 if k == 0 else 1 if k <= 4 else 2

        def scaled_before(d):
            return d + 1 - (d // KB + 1)

        x_v = x.rearrange("b (p j) h -> b p j h", j=J)
        out_v = out.rearrange("b (p j) h -> b p j h", j=J)

        block = es.enter_context(nc.Block())

        @block.sync
        def _(sp):
            sp.dma_start(xt[:, 0], x_v[0]).then_inc(x_in[0], 16)
            for i, w in enumerate((sw_gate, sw_up, sw_down)):
                sp.dma_start(w_raw[:, 0, i, :], w).then_inc(w_in[0], 16)
            sp.dma_start(xt[:, 1], x_v[1]).then_inc(x_in[1], 16)
            for n, (k0, k1) in enumerate(((1, 5), (5, 9))):
                e0, e1 = 2 * (k0 - 1), 2 * (k1 - 1)
                for i, w in enumerate((w_gate, w_up)):
                    for half in range(2):
                        sp.dma_start(w_raw[:, k0:k1, i, M * half:M * half + M],
                                     w[e0:e1].rearrange("(k s) h m -> s h k m", s=2)[half]).then_inc(w_in[1 + n], 16)
                sp.dma_start(w_raw[:, k0:k1, 2, :],
                             w_down[e0:e1].rearrange("(k s) m h -> (s m) k h", s=2)).then_inc(w_in[1 + n], 16)
                sp.dma_start(xt[:, 2 + n], x_v[2 + n]).then_inc(x_in[2 + n], 16)

            def combine_round(b):
                sp.wait_ge(combT_ready, b + 1)
                sp.dma_start(c_dram[b].rearrange("e (j p) -> (e j) p", j=J), combT[:]).then_inc(comb_out, 16)
                sp.wait_ge(comb_out, 16 * (b + 1))
                if b >= 2:
                    sp.wait_ge(act_scaled, scaled_before(KB * (b - 1) - 1))
                for half in range(2):
                    src = c_dram[b].rearrange("(k s) t -> s k t", s=2)[half:half + 1]
                    sp.dma_start(cb[M * half:M * half + M, b % 2], src.broadcast_to([M, KB - 1, S])).then_inc(cb_in[b % 2], 16)

            def store(b):
                sp.wait_ge(ot_ready, b + 1)
                sp.dma_start(out_v[b], ot[:, b % 2]).then_inc(out_done, 16)

            combine_round(0)
            combine_round(1)
            store(0)
            combine_round(2)
            store(1)
            combine_round(3)
            store(2)
            store(3)
            sp.wait_ge(out_done, 16 * NB)
            sp.wait_ge(comb_out, 16 * NB)

        @block.gpsimd
        def _(pool):
            pool.memset(ident[:], 0.0).then_inc(zeroed, 1)
            pool.memset(before[:], 1.0).then_inc(zeroed, 1)
            pool.memset(minus_half[:], -0.5).then_inc(const_ready, 1)
            pool.wait_ge(zeroed, 2)
            pool.affine_select(out=ident[:], in_=ident[:], compare_op=ALU.not_equal, fill=1.0, base=0,
                               pattern=[[-1, P]], channel_multiplier=1).then_inc(const_ready, 1)
            pool.affine_select(out=before[:], in_=before[:], compare_op=ALU.is_gt, fill=0.0, base=0,
                               pattern=[[1, NG], [-1, NG]], channel_multiplier=0).then_inc(const_ready, 1)

            norms = []

            def inv_std(b, n):
                pool.wait_ge(mv_ready[n], J * (b + 1))
                if norms:
                    pool.wait_ge(rstd_ready[norms[-1][1]], norms[-1][0] + 1)
                pool.tensor_scalar(veps[:], mv[:, n, :, 1], EPS, None, ALU.add).then_inc(veps_ready, 1)
                norms.append((b, n))
                pool.wait_ge(veps_ready, len(norms))
                if b:
                    pool.wait_ge(xn_ready[n], J * b)
                pool.tensor_tensor(rstd[:, n], veps[:], minus_half[:], ALU.pow).then_inc(rstd_ready[n], 1)

            def split_lo(k):
                pool.wait_ge(w_hi_ready, k + 1)
                pool.tensor_tensor(w_lo[:, k], w_raw[:, k], w_hi[:, k].bitcast(F32), ALU.subtract).then_inc(w_lo_ready, 1)

            def scale(d):
                b, k = divmod(d, KB)
                if k == 0:
                    return
                if k == 1:
                    pool.wait_ge(cb_in[b % 2], 32 * (b // 2 + 1))
                pool.wait_ge(act_ready, d + 1)
                pool.tensor_tensor(act[:, d % RING], act[:, d % RING], cb[:, b % 2, k - 1], ALU.mult).then_inc(act_scaled, 1)

            pool.wait_ge(const_ready, 3)
            scaled, split = 0, 0
            for i in range(FIRST, SLOTS):
                for b in range(NB):
                    if i == BASE[b] + R_RSTD1:
                        inv_std(b, 0)
                    if i == BASE[b] + R_RSTD2:
                        inv_std(b, 1)
                if i == FIRST + 2:
                    pool.wait_ge(gk_hi_ready, 1)
                    pool.tensor_tensor(gk_parts[:, 1], gk[:], gk_parts[:, 0].bitcast(F32), ALU.subtract).then_inc(gk_lo_ready, 1)
                for _ in range(W_SPLIT.get(i, 0)):
                    split_lo(split)
                    split += 1
                ahead = max(DOWNS[min(i + 2, SLOTS)], default=-1) + 1 if i >= 0 else 0
                while scaled < ahead:
                    scale(scaled)
                    scaled += 1
            while scaled < SLOTS:
                scale(scaled)
                scaled += 1

        @block.scalar
        def _(act_e):
            act_e.dma_start(gates[:, 0:1], g_xattn.partition_broadcast(P)).then_inc(small_in, 16)
            act_e.dma_start(gates[:, 1:2], g_ffn.partition_broadcast(P)).then_inc(small_in, 16)
            act_e.dma_start(bias_b[:], gate_bias.partition_broadcast(P)).then_inc(small_in, 16)
            act_e.dma_start(gk[:], gate_kernel).then_inc(small_in, 16)
            act_e.dma_start(ctx_sb[:], ctx_in.rearrange("b c h -> c b h")).then_inc(ctx_in_s, 16)
            act_e.wait_ge(warm_ready, 1)
            act_e.activation(warm[:], warm[:], ACT.Silu).then_inc(silu_warm, 1)
            act_e.wait_ge(small_in, 64)
            act_e.activation(gates_t[:], gates[:], ACT.Tanh).then_inc(gates_tanh, 1)
            act_e.activation(gk_parts[:, 0], gk[:], ACT.Copy).then_inc(gk_hi_ready, 1)
            act_e.wait_ge(ctxT_done, 1)
            act_e.activation(ctxT[:], bank_l[:, 0:NB * C].rearrange("p (b c) -> p b c", b=NB), ACT.Copy).then_inc(ctxT_ready, 1)

            def split_hi(k):
                c = w_chunk(k)
                act_e.wait_ge(w_in[c], 48 if c == 0 else 80)
                act_e.activation(w_hi[:, k], w_raw[:, k], ACT.Copy).then_inc(w_hi_ready, 1)

            def evac_xnT(b):
                act_e.wait_ge(xnT_done[0], b + 1)
                if b:
                    act_e.wait_ge(h_done, b)
                act_e.activation(xnT[:], bank_t[:], ACT.Copy).then_inc(xnT_ready, 1)

            def square_h(b):
                act_e.wait_ge(h_done, b + 1)
                if b:
                    act_e.wait_ge(z_ready, b)
                act_e.activation(hsq[:], bank_h[0:C], ACT.Square).then_inc(hsq_ready, 1)

            def tanh_z(b):
                act_e.wait_ge(z_ready, b + 1)
                if b:
                    act_e.wait_ge(aT_ready, b)
                act_e.activation(th[:], z[:], ACT.Tanh, scale=GELU_C * GELU_A).then_inc(th_ready, 1)

            def split_x_hi(b):
                act_e.wait_ge(xnT_done[1], b + 1)
                if b >= 2:
                    act_e.wait_ge(u_done, KB * (b - 1))
                    act_e.wait_ge(logits_done, b - 1)
                act_e.activation(xh[:, b % 2], bank_t[:], ACT.Copy).then_inc(xh_ready, 1)

            def tanh_logits(b):
                act_e.wait_ge(lg_ready, b + 1)
                if b:
                    act_e.wait_ge(r_step, R_ALL * (b - 1) + 1)
                act_e.activation(rth[:], lg[:], ACT.Tanh, scale=0.5).then_inc(rth_ready, 1)

            def evac_combT(b):
                act_e.wait_ge(combT_done, b + 1)
                if b:
                    act_e.wait_ge(comb_out, 16 * b)
                act_e.activation(combT[:], bank_l[0:J * E, 0:P], ACT.Copy).then_inc(combT_ready, 1)

            def silu(i):
                act_e.wait_ge(g_done, i + 1)
                if i >= 3:
                    act_e.wait_ge(act_ready, i - 2)
                act_e.activation(sg[:, i % 3], bank_g[i % 2][:], ACT.Silu).then_inc(sg_ready, 1)

            def split_act_hi(d):
                if d % KB:
                    act_e.wait_ge(act_scaled, scaled_before(d))
                else:
                    act_e.wait_ge(act_ready, d + 1)
                if d >= 2:
                    act_e.wait_ge(down_done, d - 1)
                act_e.activation(ah[:, d % 2], act[:, d % RING], ACT.Copy).then_inc(ah_ready, 1)

            def evac_y(b):
                act_e.wait_ge(down_done, KB * (b + 1))
                if b:
                    act_e.wait_ge(yT_done, b)
                act_e.activation(yT[:], bank_y[:], ACT.Copy, scale=gates_t[:, 1:2]).then_inc(y_ready, 1)

            split = 0
            for i in range(FIRST, LAST):
                if 0 <= i < SLOTS:
                    silu(i)
                for b in range(NB):
                    if i == BASE[b] + R_T1:
                        evac_xnT(b)
                    if i == BASE[b] + R_HIDDEN:
                        square_h(b)
                    if i == BASE[b] + R_GELU:
                        tanh_z(b)
                    if i == BASE[b] + R_T2:
                        split_x_hi(b)
                    if i == BASE[b] + R_LOGITS:
                        tanh_logits(b)
                    if i == CT_SLOT[b]:
                        evac_combT(b)
                    if i == Y_SLOT[b]:
                        evac_y(b)
                for _ in range(W_SPLIT.get(i, 0)):
                    split_hi(split)
                    split += 1
                if 0 <= i < SLOTS:
                    for d in DOWNS[i + 1]:
                        split_act_hi(d)

        @block.vector
        def _(dve):
            norms = []

            def layer_stats(b, n):
                if n == 0:
                    dve.wait_ge(x_in[b], 16)
                else:
                    dve.wait_ge(x2_ready, b + 1)
                if norms:
                    dve.wait_ge(mv_ready[norms[-1][1]], J * (norms[-1][0] + 1))
                for j in range(J):
                    dve.bn_stats(stats[:, j], xt[:, b, j]).then_inc(stats_done, 1)
                if b:
                    dve.wait_ge(rstd_ready[n], b)
                for j in range(J):
                    dve.wait_ge(stats_done, J * len(norms) + j + 1)
                    dve.bn_aggr(mv[:, n, j], stats[:, j]).then_inc(mv_ready[n], 1)
                norms.append((b, n))

            def normalise(b, n):
                dve.wait_ge(rstd_ready[n], b + 1)
                dve.wait_ge(mv_ready[n], J * (b + 1))
                if b:
                    dve.wait_ge(xnT_done[n], b)
                for j in range(J):
                    dve.tensor_scalar(xn[:, n, j], xt[:, b, j], mv[:, n, j, 0:1], rstd[:, n, j:j + 1],
                                      ALU.subtract, ALU.mult).then_inc(xn_ready[n], 1)

            def gelu_z(b):
                dve.wait_ge(hsq_ready, b + 1)
                if b:
                    dve.wait_ge(th_ready, b)
                dve.scalar_tensor_tensor(z[:], hsq[:], 1.0 / GELU_A, bank_h[0:C], ALU.add, ALU.mult).then_inc(z_ready, 1)

            def gelu_a(b):
                dve.wait_ge(th_ready, b + 1)
                if b:
                    dve.wait_ge(attn_done, b)
                dve.scalar_tensor_tensor(aT[:], th[:], 1.0, bank_h[0:C], ALU.add, ALU.mult).then_inc(aT_ready, 1)

            def residual(b):
                dve.wait_ge(attn_done, b + 1)
                dve.wait_ge(gates_ready, 1)
                dve.scalar_tensor_tensor(xt[:, b], bank_h[:].rearrange("p (j h) -> p j h", j=J), gx_half[:, 0:1], xt[:, b],
                                         ALU.mult, ALU.add).then_inc(x2_ready, 1)

            def split_x_lo(b):
                dve.wait_ge(xh_ready, b + 1)
                dve.tensor_tensor(xl[:, b % 2], bank_t[:], xh[:, b % 2].bitcast(F32), ALU.subtract).then_inc(xl_ready, 1)

            def router(b, n):
                done = R_ALL * b + sum(R_OPS[:n])
                if done and n:
                    dve.wait_ge(r_step, done)
                masked_v = masked[:].rearrange("p j e -> p (j e)").rearrange("p (g e) -> p g e", e=EG)
                sfc_v = sfc[:].rearrange("p j e -> p (j e)").rearrange("p (g e) -> p g e", e=EG)
                pairs = sfc[:].rearrange("p j e -> p (j e)").rearrange("p (q r) -> p r q", r=2)
                if n == 0:
                    dve.wait_ge(logits_done, b + 1)
                    if b:
                        dve.wait_ge(rth_ready, b)
                    dve.tensor_reduce(lg[:].rearrange("p (j e) -> p j e", j=J),
                                      bank_l[:, 0:J * 2 * E].rearrange("p (j s e) -> p j e s", j=J, s=2), AX.X, ALU.add).then_inc(lg_ready, 1)
                elif n == 1:
                    dve.wait_ge(rth_ready, b + 1)
                    dve.scalar_tensor_tensor(sfc[:, :, 0:E], rth[:].rearrange("p (j e) -> p j e", j=J), 0.5,
                                             bias_h[:].unsqueeze(1).broadcast_to([P, J, E]), ALU.mult, ALU.add).then_inc(r_step, 1)
                elif n == 2:
                    dve.tensor_tensor(pmax[:], pairs[:, 0], pairs[:, 1], ALU.max).then_inc(r_step, 1)
                    dve.tensor_tensor(pmin[:], pairs[:, 0], pairs[:, 1], ALU.min).then_inc(r_step, 1)
                elif n == 3:
                    mx = pmax[:].rearrange("p (q r) -> p r q", r=2)
                    mn = pmin[:].rearrange("p (q r) -> p r q", r=2)
                    dve.tensor_tensor(top[:], mx[:, 0], mx[:, 1], ALU.max).then_inc(r_step, 1)
                    dve.tensor_tensor(sec_a[:], mx[:, 0], mx[:, 1], ALU.min).then_inc(r_step, 1)
                    dve.tensor_tensor(sec_b[:], mn[:, 0], mn[:, 1], ALU.max).then_inc(r_step, 1)
                elif n == 4:
                    dve.tensor_tensor(sec[:], sec_a[:], sec_b[:], ALU.max).then_inc(r_step, 1)
                elif n == 5:
                    dve.tensor_tensor(gs[:].rearrange("p j g -> p (j g)"), top[:], sec[:], ALU.add).then_inc(r_step, 1)
                elif n == 6:
                    other = gs[:, :, 0:NG].unsqueeze(2).broadcast_to([P, J, NG, NG])
                    own = gs[:, :, 0:NG].unsqueeze(3).broadcast_to([P, J, NG, NG])
                    dve.tensor_tensor(gt[:], other, own, ALU.is_gt).then_inc(r_step, 1)
                    dve.tensor_tensor(eq[:], other, own, ALU.is_equal).then_inc(r_step, 1)
                elif n == 7:
                    dve.tensor_tensor(eq[:], eq[:], before[:].unsqueeze(1).broadcast_to([P, J, NG, NG]), ALU.mult).then_inc(r_step, 1)
                elif n == 8:
                    dve.tensor_tensor(gt[:], gt[:], eq[:], ALU.add).then_inc(r_step, 1)
                elif n == 9:
                    dve.tensor_reduce(rank[:, :, 0:NG], gt[:], AX.X, ALU.add).then_inc(r_step, 1)
                elif n == 10:
                    dve.scalar_tensor_tensor(masked_v, rank[:].rearrange("p j g -> p (j g)").unsqueeze(2).broadcast_to([P, J * (NG + 1), EG]),
                                             float(TOPG), sfc_v, ALU.is_lt, ALU.mult).then_inc(r_step, 1)
                elif n == 11:
                    for j in range(J):
                        dve.max(top8[:, j], masked[:, j]).then_inc(r_step, 1)
                elif n == 12:
                    for j in range(J):
                        dve.match_replace(rep[:, j], top8[:, j], masked[:, j], PICKED).then_inc(r_step, 1)
                    dve.tensor_reduce(den[:], top8[:, :, EG:8], AX.X, ALU.add).then_inc(r_step, 1)
                elif n == 13:
                    dve.tensor_scalar(den2[:], den[:], 1e-20, 1.0 / ROUTE_SCALE, ALU.add, ALU.mult).then_inc(r_step, 1)
                    dve.scalar_tensor_tensor(num[:], rep[:, :, 0:E], PICKED, masked[:, :, 0:E], ALU.is_equal, ALU.mult).then_inc(r_step, 1)
                elif n == 14:
                    dve.reciprocal(rec[:], den2[:]).then_inc(r_step, 1)
                elif n == 15:
                    if b:
                        dve.wait_ge(combT_done, b)
                    dve.tensor_tensor(comb[:].rearrange("p e j -> p j e"), num[:], rec[:].unsqueeze(2).broadcast_to([P, J, E]), ALU.mult).then_inc(r_step, 1)

            def gate_up(i):
                dve.wait_ge(sg_ready, i + 1)
                dve.wait_ge(u_done, i + 1)
                if i >= RING:
                    dve.wait_ge(al_ready, i - RING + 1)
                dve.tensor_tensor(act[:, i % RING], sg[:, i % 3], bank_u[i % 2][:], ALU.mult).then_inc(act_ready, 1)

            def split_act_lo(d):
                dve.wait_ge(ah_ready, d + 1)
                dve.tensor_tensor(al[:, d % 2], act[:, d % RING], ah[:, d % 2].bitcast(F32), ALU.subtract).then_inc(al_ready, 1)

            def finish(b):
                dve.wait_ge(yT_done, b + 1)
                if b >= 2:
                    dve.wait_ge(out_done, 16 * (b - 1))
                dve.tensor_tensor(ot[:, b % 2], bank_t[:].rearrange("p (j h) -> p j h", j=J), xt[:, b], ALU.add).then_inc(ot_ready, 1)

            dve.memset(sfc[:], BIG).then_inc(sentinels, 1)
            dve.memset(rank[:], 0.0).then_inc(sentinels, 1)
            dve.memset(warm[:], 0.0).then_inc(warm_ready, 1)
            dve.wait_ge(sentinels, 2)
            for i in range(FIRST, LAST):
                if i == BASE[0] + R_T1:
                    dve.wait_ge(gates_tanh, 1)
                    dve.tensor_scalar(gx_half[:], gates_t[:, 0:1], 0.5, None, ALU.mult).then_inc(gates_ready, 1)
                    dve.tensor_scalar(bias_h[:], bias_b[:], 0.5, None, ALU.add).then_inc(bias_ready, 1)
                    dve.wait_ge(bias_ready, 1)
                steps = [(b, n) for b in range(NB) for n in R_SLOTS[b].get(i, [])]
                if steps:
                    router(*steps[0])
                if 0 <= i < SLOTS:
                    gate_up(i)
                for s in steps[1:2]:
                    router(*s)
                for b in range(NB):
                    if i == BASE[b] + R_STATS1:
                        layer_stats(b, 0)
                    if i == BASE[b] + R_NORM1:
                        normalise(b, 0)
                    if i == BASE[b] + R_HIDDEN:
                        gelu_z(b)
                    if i == BASE[b] + R_GELU:
                        gelu_a(b)
                    if i == BASE[b] + R_ATTEND:
                        residual(b)
                        layer_stats(b, 1)
                    if i == BASE[b] + R_NORM2:
                        normalise(b, 1)
                    if i == BASE[b] + R_T2:
                        split_x_lo(b)
                    if i == YT_SLOT[b]:
                        finish(b)
                if 0 <= i < SLOTS:
                    for d in DOWNS[i + 1]:
                        split_act_lo(d)
                for s in steps[2:]:
                    router(*s)

        @block.tensor
        def _(pe):
            reader = {"t": None, "h": None, "l": (ctxT_ready, 1)}

            def free(bank):
                if reader[bank]:
                    pe.wait_ge(*reader[bank])

            def transpose_xn(b, n):
                pe.wait_ge(xn_ready[n], J * (b + 1))
                free("t")
                for j in range(J):
                    last = pe.transpose(bank_t[:, j * P:(j + 1) * P], xn[:, n, j], ident[:])
                last.then_inc(xnT_done[n], 1)
                reader["t"] = (xl_ready if n else xnT_ready, b + 1)

            def hidden(b):
                pe.wait_ge(xnT_ready, b + 1)
                free("h")
                pe.matmul(bank_h[0:C], ctxT[:, b], xnT[:], start=True, stop=True).then_inc(h_done, 1)
                reader["h"] = (aT_ready, b + 1)

            def attend(b):
                pe.wait_ge(aT_ready, b + 1)
                for j in range(J):
                    last = pe.matmul(bank_h[:, j * H:(j + 1) * H], aT[:, j * P:(j + 1) * P], ctx_sb[:, b], start=True, stop=True)
                last.then_inc(attn_done, 1)
                reader["h"] = (x2_ready, b + 1)

            def logits(b):
                pe.wait_ge(xl_ready, b + 1)
                free("l")
                for j in range(J):
                    o = bank_l[:, 2 * E * j:2 * E * (j + 1)]
                    t = slice(j * P, (j + 1) * P)
                    parts = gk_parts[:].rearrange("p s e -> p (s e)")
                    pe.matmul(o, xh[:, b % 2, t], parts, start=True, stop=False)
                    last = pe.matmul(o, xl[:, b % 2, t], parts, start=False, stop=True)
                last.then_inc(logits_done, 1)
                reader["l"] = (lg_ready, b + 1)

            def transpose_comb(b):
                pe.wait_ge(r_step, R_ALL * (b + 1))
                free("l")
                pe.transpose(bank_l[0:J * E, 0:P], comb[:].rearrange("p e j -> p (e j)"), ident[:]).then_inc(combT_done, 1)
                reader["l"] = (combT_ready, b + 1)

            def three(o, k, i, hi, lo, start, stop):
                pe.matmul(o, w_lo[:, k, i], hi, start=start, stop=False)
                pe.matmul(o, w_hi[:, k, i], hi, start=False, stop=False)
                return pe.matmul(o, w_hi[:, k, i], lo, start=False, stop=stop)

            def gate_up(i):
                b, k = divmod(i, KB)
                if k == 0:
                    pe.wait_ge(xl_ready, b + 1)
                if b == 0:
                    pe.wait_ge(w_lo_ready, k + 1)
                if i >= 2:
                    pe.wait_ge(act_ready, i - 1)
                hi, lo = xh[:, b % 2], xl[:, b % 2]
                three(bank_g[i % 2][:], k, 0, hi, lo, True, True).then_inc(g_done, 1)
                three(bank_u[i % 2][:], k, 1, hi, lo, True, True).then_inc(u_done, 1)

            def down(d):
                b, k = divmod(d, KB)
                pe.wait_ge(al_ready, d + 1)
                if k == 0 and b:
                    pe.wait_ge(y_ready, b)
                three(bank_y[:], k, 2, ah[:, d % 2], al[:, d % 2], k == 0, k == KB - 1).then_inc(down_done, 1)

            def transpose_y(b):
                pe.wait_ge(y_ready, b + 1)
                free("t")
                for j in range(J):
                    last = pe.transpose(bank_t[:, j * H:(j + 1) * H], yT[:, j * P:(j + 1) * P], ident[:])
                last.then_inc(yT_done, 1)
                reader["t"] = (ot_ready, b + 1)

            pe.wait_ge(const_ready, 3)
            pe.wait_ge(ctx_in_s, 16)
            for b in range(NB):
                last = pe.transpose(bank_l[:, b * C:(b + 1) * C], ctx_sb[:, b], ident[0:C, 0:C])
            last.then_inc(ctxT_done, 1)
            for i in range(FIRST, LAST):
                if 0 <= i < SLOTS:
                    gate_up(i)
                for b in range(NB):
                    if i == BASE[b] + R_T1:
                        transpose_xn(b, 0)
                    if i == BASE[b] + R_HIDDEN:
                        if b == 0:
                            pe.wait_ge(ctxT_ready, 1)
                        hidden(b)
                    if i == BASE[b] + R_ATTEND:
                        attend(b)
                    if i == BASE[b] + R_T2:
                        transpose_xn(b, 1)
                    if i == BASE[b] + R_LOGITS:
                        if b == 0:
                            pe.wait_ge(gk_lo_ready, 1)
                        logits(b)
                    if i == CT_SLOT[b]:
                        transpose_comb(b)
                    if i == YT_SLOT[b]:
                        transpose_y(b)
                if 0 <= i <= SLOTS:
                    for d in DOWNS[i]:
                        down(d)


_INS = ['x', 'ctx_1024', 'g_xattn', 'g_ffn', 'L0_ffn_gate_kernel', 'L0_ffn_gate_bias', 'L0_ffn_w_gate', 'L0_ffn_w_up',
        'L0_ffn_w_down', 'L0_ffn_sw_gate', 'L0_ffn_sw_up', 'L0_ffn_sw_down']


def kernel(**inputs):
    import numpy as _np
    import concourse.bacc as _bacc
    from concourse import mybir as _mybir
    from concourse.bass_utils import run_bass_kernel_spmd as _run

    nc = _bacc.Bacc("TRN2", target_bir_lowering=False, num_devices=1)
    arrays, args = {}, []
    for name in _INS:
        a = _np.ascontiguousarray(inputs[name])
        arrays[f"in_{name}_dram"] = a
        args.append(nc.dram_tensor(f"in_{name}_dram", a.shape, _mybir.dt.from_np(a.dtype), kind="ExternalInput").ap())
    args.append(nc.dram_tensor("combine_weights", (NB, E, S), F32, kind="Internal").ap())
    args.append(nc.dram_tensor("out_0_dram", (NB, S, H), F32, kind="ExternalOutput").ap())
    flamingo_block(nc, *args)
    r = _run(nc, [arrays], core_ids=[0])
    return r.results[0]["out_0_dram"]
```

```python
from contextlib import ExitStack

import concourse.bass as bass
from concourse import mybir

ALU = mybir.AluOpType
ACT = mybir.ActivationFunctionType
AX = mybir.AxisListType
F32 = mybir.dt.float32
F32R = mybir.dt.float32r

P = 128
NB = 4
S = 512
J = S // P
H = 128
C = 77
E = 16
M = 64
NG = 4
EG = E // NG
TOPG = 2
TOPK = 4
EX = E + EG
ROUTE_SCALE = 2.5
KB = 1 + E * M // P
SLOTS = NB * KB
EPS = 1e-5
BIG = 1e30
PICKED = -1e30
GELU_C = 0.7978845608028654
GELU_A = 0.044715
RING = 18

Q = 4
LAG = [8, 8, 9, 8, 9, 8, 8, 7, 7, 7, 6, 6, 6, 5, 5, 5, 5, 5, 5, 5, 4, 4, 4, 3, 3, 2, 2, 4, 4, 4, 3, 3, 3, 2, 2, 1]
UNITS = [(0, 0, J // 2), (0, J // 2, J)] + [(b, 0, J) for b in range(1, NB)]
OUTS = [(b, 0, J) for b in range(NB - 1)] + [(NB - 1, 0, J // 2), (NB - 1, J // 2, J)]
AT = {
    "ctxT": [-68],
    "keep_warm": [-31, -20, -20, -18, -16, -16, -10, -5, -5, -2],
    "small": [-24],
    "small_dve": [-19],
    "gk_lo": [-21],
    "w_hi": [-19, -16, -16, -8, -8, -3, 2, 2, 10],
    "w_lo": [-21, -14, -3, -2, -1, 1, 7, 13, 13],
    "stats1": [-66, -48, -35, -6, 22],
    "rstd1": [-58, -52, -30, -1, 29],
    "norm1_dve": [-41, -36],
    "norm1": [None, None, -17, 8, 46],
    "T1": [-41, -30, -9, 13, 54],
    "xnT": [-43, -25, -13, 13, 53],
    "h": [-31, -22, -5, 14, 56],
    "square": [-28, -21, -5, 14, 57],
    "z": [-22, -19, 0, 15, 58],
    "tanh": [-25, -18, -2, 22, 58],
    "a": [-20, -16, 2, 22, 60],
    "attend": [-21, -14, 11, 29, 64],
    "residual": [-17, -10, 10, 32, 65],
    "stats2": [-15, -7, 10, 33, 68],
    "rstd2": [-14, -5, 18, 26, 63],
    "norm2_dve": [-7, -5],
    "norm2": [None, None, 14, 36, 72],
    "T2": [-3, -3, 20, 41, 78],
    "x_hi": [-6, -5, 21, 44, 75],
    "x_lo": [-2, -1, 22, 44, 75],
    "logits_pe": [2, 27, 49, 83],
    "logits_dve": [4, 23, 50, 80],
    "logits": [4, 25, 51, 82],
    "router": [8, 28, 51, 82],
    "combT_pe": [22, 44, 71, 100],
    "combT": [22, 44, 69, 104],
    "y": [63, 91, 119, 163, 174],
    "yT": [68, 93, 124, 169, 183],
    "finish": [71, 103, 128, 155, 158],
}
ROUTER_PACE = [3, 4, 3, 5]
WHOLE = range(34, SLOTS)
GATE_UP_AT, DOWN_AT = 0, 3
SILU_AT, HI_AT = 0, 1
MUL_AT, LO_AT = 2, 3
SCALE_AT, SCALE_AHEAD = 0, 4
CB_CHUNKS = ((1, 2), (2, 3), (3, 5), (5, KB))
WARM_UP = 7


def plan_downs():
    out, slot = [[] for _ in range(SLOTS + 1)], 0
    for d in range(SLOTS):
        slot = min(max(slot, d + LAG[d]), SLOTS)
        out[slot].append(d)
    return out


DOWNS = plan_downs()
assert not any({KB * b - 1, KB * b} <= set(downs) for b in range(1, NB) for downs in DOWNS)

LAST_UNIT = [max(u for u, (b, _, _) in enumerate(UNITS) if b == n) for n in range(NB)]
REUSES = [u for u in range(len(UNITS)) if UNITS[u][0] > 0]
TICKS = [t for at in AT.values() for t in at if t is not None]
FIRST = min(TICKS)
LAST = max(max(TICKS) + 1, Q * (SLOTS + 1))

R_OPS = [0, 1, 2, 3, 1, 1, 2, 1, 1, 1, 1, 4, 5, 2, 1, 1]
R_ALL = sum(R_OPS)


def now(step, t):
    return [n for n, at in enumerate(AT[step]) if at == t]


def router_steps(b, t):
    steps = [0] if AT["logits_dve"][b] == t else []
    return steps + [n for n in range(1, len(R_OPS)) if AT["router"][b] + (n - 1) * ROUTER_PACE[b] // 4 == t]


def slot_at(t, phase):
    i, p = divmod(t, Q)
    return [i] if p == phase and 0 <= i <= SLOTS else []


def place(slot):
    b, n = divmod(slot, KB)
    return b, (n + 1) % KB if b == NB - 1 else n


def flamingo_block(nc, x, ctx_in, g_xattn, g_ffn, gate_kernel, gate_bias, w_gate, w_up, w_down,
                   sw_gate, sw_up, sw_down, c_dram, out):
    with ExitStack() as es:
        def sb(name, shape, dt=F32):
            return es.enter_context(nc.sbuf_tensor(name, shape, dt))

        def bank(name):
            return es.enter_context(nc.psum_tensor(name, [P, S], F32))

        def sem(name):
            return es.enter_context(nc.semaphore(name))

        ident = sb("ident", [P, P])
        before = sb("before", [P, NG, NG])
        minus_half = sb("minus_half", [P, J])
        warm = sb("warm", [P, 1])
        ctx_sb = sb("ctx_sb", [C, NB, H])
        ctxT = sb("ctxT", [P, NB, C])
        gates = sb("gates", [P, 2])
        gates_t = sb("gates_t", [P, 2])
        gx_half = sb("gx_half", [P, 1])
        bias_b = sb("bias_b", [P, E])
        bias_h = sb("bias_h", [P, E])
        gk = sb("gk", [P, E])
        gk_parts = sb("gk_parts", [P, 2, E], F32R)
        w_raw = sb("w_raw", [P, KB, 3, P])
        w_hi = sb("w_hi", [P, KB, 3, P], F32R)
        w_lo = sb("w_lo", [P, KB, 3, P], F32R)

        xt = sb("xt", [P, NB, J, H])
        stats = sb("stats", [P, 2, J, 6])
        mv = sb("mv", [P, 2, J, 2])
        veps = sb("veps", [P, J])
        rstd = sb("rstd", [P, 2, J])
        negm = sb("negm", [P, J])
        nmr = sb("nmr", [P, 2, J])
        xn = sb("xn", [P, 2, J, H])
        xnT = sb("xnT", [P, S])
        hsq = sb("hsq", [C, S])
        z = sb("z", [C, S])
        th = sb("th", [C, S])
        aT = sb("aT", [C, S])
        xh = sb("xh", [P, 2, S], F32R)
        xl = sb("xl", [P, 2, S], F32R)
        yT = sb("yT", [P, S])
        ot = sb("ot", [P, 2, J, H])

        lg = sb("lg", [P, J * E])
        rth = sb("rth", [P, J * E])
        sfc = sb("sfc", [P, J, EX])
        pmax = sb("pmax", [P, J * EX // 2])
        pmin = sb("pmin", [P, J * EX // 2])
        top = sb("top", [P, J * (NG + 1)])
        sec_a = sb("sec_a", [P, J * (NG + 1)])
        sec_b = sb("sec_b", [P, J * (NG + 1)])
        sec = sb("sec", [P, J * (NG + 1)])
        gs = sb("gs", [P, J, NG + 1])
        gt = sb("gt", [P, J, NG, NG])
        eq = sb("eq", [P, J, NG, NG])
        rank = sb("rank", [P, J, NG + 1])
        masked = sb("masked", [P, J, EX])
        top8 = sb("top8", [P, J, 8])
        rep = sb("rep", [P, J, EX])
        num = sb("num", [P, J, E])
        den = sb("den", [P, J])
        den2 = sb("den2", [P, J])
        rec = sb("rec", [P, J])
        comb = sb("comb", [P, E, J])
        combT = sb("combT", [E * J, P])
        cb = sb("cb", [P, 2, KB - 1, S])

        sg = sb("sg", [P, 3, S])
        act = sb("act", [P, RING, S])
        ah = sb("ah", [P, 2, S], F32R)
        al = sb("al", [P, 2, S], F32R)

        bank_g = [bank("bank_g0"), bank("bank_g1")]
        bank_u = [bank("bank_u0"), bank("bank_u1")]
        bank_t = bank("bank_t")
        bank_h = bank("bank_h")
        bank_l = bank("bank_l")
        bank_y = bank("bank_y")

        x_in = [sem(f"x_in{u}") for u in range(len(UNITS))]
        ctx_in_s, small_in = sem("ctx_in"), sem("small_in")
        w_in = [sem(f"w_in{n}") for n in range(3)]
        zeroed, const_ready, sentinels = sem("zeroed"), sem("const_ready"), sem("sentinels")
        gates_tanh, gates_ready, bias_ready = sem("gates_tanh"), sem("gates_ready"), sem("bias_ready")
        gk_hi_ready, gk_lo_ready = sem("gk_hi_ready"), sem("gk_lo_ready")
        w_hi_ready, w_lo_ready = sem("w_hi_ready"), sem("w_lo_ready")
        ctxT_done, ctxT_ready = sem("ctxT_done"), sem("ctxT_ready")
        stats_done, mv_ready = sem("stats_done"), [sem("mv1_ready"), sem("mv2_ready")]
        veps_ready, rstd_ready = sem("veps_ready"), [sem("rstd1_ready"), sem("rstd2_ready")]
        xn_first = [sem("xn1_first"), sem("xn2_first")]
        xn_ready = [sem("xn1_ready"), sem("xn2_ready")]
        xnT_done = [sem("xn1T_done"), sem("xn2T_done")]
        negm_ready, nmr_ready = sem("negm_ready"), [sem("nmr1_ready"), sem("nmr2_ready")]
        xnT_ready = sem("xnT_ready")
        lg_ready = sem("lg_ready")
        warm_ready, silu_warm = sem("warm_ready"), sem("silu_warm")
        xh_ready, xl_ready = sem("xh_ready"), sem("xl_ready")
        h_done, hsq_ready, z_ready, th_ready, aT_ready = sem("h_done"), sem("hsq_ready"), sem("z_ready"), sem("th_ready"), sem("aT_ready")
        attn_done, x2_ready = sem("attn_done"), sem("x2_ready")
        logits_done, rth_ready, r_step = sem("logits_done"), sem("rth_ready"), sem("r_step")
        combT_done, combT_ready, comb_out, cb_in = sem("combT_done"), sem("combT_ready"), sem("comb_out"), [[sem(f"cb_in{par}{n}") for n in range(len(CB_CHUNKS))] for par in range(2)]
        g_done, u_done, sg_ready, act_ready, act_scaled = sem("g_done"), sem("u_done"), sem("sg_ready"), sem("act_ready"), sem("act_scaled")
        ah_ready, al_ready, down_done = sem("ah_ready"), sem("al_ready"), sem("down_done")
        y_ready, yT_done, ot_ready, out_done = sem("y_ready"), sem("yT_done"), sem("ot_ready"), sem("out_done")

        def w_chunk(k):
            return 0 if k == 0 else 1 if k <= 4 else 2

        def scaled_before(d):
            return sum(1 for n in range(d + 1) if place(n)[1])

        def tokens(u):
            return slice(UNITS[u][1] * P, UNITS[u][2] * P)

        def side_t(u):
            return bank_g[1] if u == 1 else bank_t

        def side_h(u):
            return bank_u[1] if u == 1 else bank_h

        def side_y(v):
            return bank_h if v == len(OUTS) - 1 else bank_t

        x_v = x.rearrange("b (p j) h -> b p j h", j=J)
        out_v = out.rearrange("b (p j) h -> b p j h", j=J)

        block = es.enter_context(nc.Block())

        @block.sync
        def _(sp):
            for u in range(2):
                _, j0, j1 = UNITS[u]
                sp.dma_start(xt[:, 0, j0:j1], x_v[0][:, j0:j1]).then_inc(x_in[u], 16)
            sp.dma_start(gates[:, 0:1], g_xattn.partition_broadcast(P)).then_inc(small_in, 16)
            sp.dma_start(gates[:, 1:2], g_ffn.partition_broadcast(P)).then_inc(small_in, 16)
            sp.dma_start(bias_b[:], gate_bias.partition_broadcast(P)).then_inc(small_in, 16)
            sp.dma_start(gk[:], gate_kernel).then_inc(small_in, 16)
            sp.dma_start(xt[:, 1], x_v[1]).then_inc(x_in[2], 16)
            for i, w in enumerate((sw_gate, sw_up, sw_down)):
                sp.dma_start(w_raw[:, 0, i, :], w).then_inc(w_in[0], 16)
            for n, (k0, k1) in enumerate(((1, 5), (5, 9))):
                e0, e1 = 2 * (k0 - 1), 2 * (k1 - 1)
                for i, w in enumerate((w_gate, w_up)):
                    for half in range(2):
                        sp.dma_start(w_raw[:, k0:k1, i, M * half:M * half + M],
                                     w[e0:e1].rearrange("(k s) h m -> s h k m", s=2)[half]).then_inc(w_in[1 + n], 16)
                sp.dma_start(w_raw[:, k0:k1, 2, :],
                             w_down[e0:e1].rearrange("(k s) m h -> (s m) k h", s=2)).then_inc(w_in[1 + n], 16)
                sp.dma_start(xt[:, 2 + n], x_v[2 + n]).then_inc(x_in[3 + n], 16)

            def combine_round(b):
                sp.wait_ge(combT_ready, b + 1)
                sp.dma_start(c_dram[b].rearrange("e (j p) -> (e j) p", j=J), combT[:]).then_inc(comb_out, 16)
                sp.wait_ge(comb_out, 16 * (b + 1))
                if b >= 2:
                    sp.wait_ge(act_scaled, scaled_before(KB * (b - 1) - 1))
                for n, (k0, k1) in enumerate(CB_CHUNKS):
                    for half in range(2):
                        src = c_dram[b].rearrange("(k s) t -> s k t", s=2)[half:half + 1, k0 - 1:k1 - 1]
                        sp.dma_start(cb[M * half:M * half + M, b % 2, k0 - 1:k1 - 1],
                                     src.broadcast_to([M, k1 - k0, S])).then_inc(cb_in[b % 2][n], 16)

            def store(v):
                b, j0, j1 = OUTS[v]
                sp.wait_ge(ot_ready, v + 1)
                sp.dma_start(out_v[b][:, j0:j1], ot[:, b % 2, j0:j1]).then_inc(out_done, 16)

            combine_round(0)
            combine_round(1)
            store(0)
            combine_round(2)
            store(1)
            combine_round(3)
            store(2)
            store(3)
            store(4)
            sp.wait_ge(out_done, 16 * len(OUTS))

        @block.gpsimd
        def _(pool):
            pool.memset(ident[:], 0.0).then_inc(zeroed, 1)
            pool.memset(before[:], 1.0).then_inc(zeroed, 1)
            pool.memset(minus_half[:], -0.5).then_inc(const_ready, 1)
            pool.wait_ge(zeroed, 2)
            pool.affine_select(out=ident[:], in_=ident[:], compare_op=ALU.not_equal, fill=1.0, base=0,
                               pattern=[[-1, P]], channel_multiplier=1).then_inc(const_ready, 1)
            pool.affine_select(out=before[:], in_=before[:], compare_op=ALU.is_gt, fill=0.0, base=0,
                               pattern=[[1, NG], [-1, NG]], channel_multiplier=0).then_inc(const_ready, 1)

            norms = []

            def inv_std(u, n):
                b, j0, j1 = UNITS[u]
                t = slice(j0, j1)
                pool.wait_ge(mv_ready[n], J * b + j1)
                if norms:
                    pool.wait_ge(rstd_ready[norms[-1][1]], norms[-1][0] + 1)
                pool.tensor_scalar(veps[:, t], mv[:, n, t, 1], EPS, None, ALU.add).then_inc(veps_ready, 1)
                if u in REUSES:
                    wide = [v for v in norms if v[0] in REUSES]
                    if wide:
                        pool.wait_ge(nmr_ready[wide[-1][1]], wide[-1][0] - REUSES[0] + 1)
                    pool.tensor_scalar(negm[:], mv[:, n, :, 0], -1.0, None, ALU.mult).then_inc(negm_ready, 1)
                norms.append((u, n))
                pool.wait_ge(veps_ready, len(norms))
                if u == REUSES[0]:
                    pool.wait_ge(xn_first[n], J)
                elif u in REUSES:
                    pool.wait_ge(xn_ready[n], J * (b - 1))
                pool.tensor_tensor(rstd[:, n, t], veps[:, t], minus_half[:, t], ALU.pow).then_inc(rstd_ready[n], 1)
                if u in REUSES:
                    pool.wait_ge(negm_ready, len([v for v in norms if v[0] in REUSES]))
                    pool.wait_ge(rstd_ready[n], u + 1)
                    pool.tensor_tensor(nmr[:, n], negm[:], rstd[:, n], ALU.mult).then_inc(nmr_ready[n], 1)

            def split_lo(k):
                pool.wait_ge(w_hi_ready, k + 1)
                pool.tensor_tensor(w_lo[:, k], w_raw[:, k], w_hi[:, k].bitcast(F32), ALU.subtract).then_inc(w_lo_ready, 1)

            def scale(d):
                b, k = place(d)
                if k == 0:
                    return
                for n, (k0, _) in enumerate(CB_CHUNKS):
                    if k == k0:
                        pool.wait_ge(cb_in[b % 2][n], 32 * (b // 2 + 1))
                pool.wait_ge(act_ready, d + 1)
                pool.tensor_tensor(act[:, d % RING], act[:, d % RING], cb[:, b % 2, k - 1], ALU.mult).then_inc(act_scaled, 1)

            pool.wait_ge(const_ready, 3)
            scaled = 0
            for t in range(FIRST, LAST):
                for u in now("rstd2", t):
                    inv_std(u, 1)
                for u in now("rstd1", t):
                    inv_std(u, 0)
                for _ in now("gk_lo", t):
                    pool.wait_ge(gk_hi_ready, 1)
                    pool.tensor_tensor(gk_parts[:, 1], gk[:], gk_parts[:, 0].bitcast(F32), ALU.subtract).then_inc(gk_lo_ready, 1)
                for k in now("w_lo", t):
                    split_lo(k)
                for i in slot_at(t, SCALE_AT):
                    ahead = max(DOWNS[min(i + SCALE_AHEAD, SLOTS)], default=-1) + 1
                    for d in range(scaled, ahead):
                        scale(d)
                    scaled = max(scaled, ahead)

        @block.scalar
        def _(act_e):
            act_e.dma_start(ctx_sb[:], ctx_in.rearrange("b c h -> c b h")).then_inc(ctx_in_s, 16)
            act_e.wait_ge(warm_ready, 1)
            act_e.activation(warm[:], warm[:], ACT.Silu).then_inc(silu_warm, 1)

            def evac_ctxT():
                act_e.wait_ge(ctxT_done, 1)
                act_e.activation(ctxT[:], bank_l[:, 0:NB * C].rearrange("p (b c) -> p b c", b=NB), ACT.Copy).then_inc(ctxT_ready, 1)

            def split_hi(k):
                c = w_chunk(k)
                act_e.wait_ge(w_in[c], 48 if c == 0 else 80)
                act_e.activation(w_hi[:, k], w_raw[:, k], ACT.Copy).then_inc(w_hi_ready, 1)

            def small_inputs():
                act_e.wait_ge(small_in, 64)
                act_e.activation(gates_t[:], gates[:], ACT.Tanh).then_inc(gates_tanh, 1)
                act_e.activation(gk_parts[:, 0], gk[:], ACT.Copy).then_inc(gk_hi_ready, 1)

            def normalise(u, n):
                b = UNITS[u][0]
                act_e.wait_ge(nmr_ready[n], b)
                act_e.wait_ge(xnT_done[n], u)
                for j in range(J):
                    act_e.activation(xn[:, n, j], xt[:, b, j], ACT.Identity, scale=rstd[:, n, j:j + 1],
                                     bias=nmr[:, n, j:j + 1]).then_inc(xn_ready[n], 1)

            def evac_xnT(u):
                act_e.wait_ge(xnT_done[0], u + 1)
                if u in REUSES:
                    act_e.wait_ge(h_done, u)
                t = tokens(u)
                act_e.activation(xnT[:, t], side_t(u)[:, t], ACT.Copy).then_inc(xnT_ready, 1)

            def square_h(u):
                act_e.wait_ge(h_done, u + 1)
                if u in REUSES:
                    act_e.wait_ge(z_ready, u)
                t = tokens(u)
                act_e.activation(hsq[:, t], side_h(u)[0:C, t], ACT.Square).then_inc(hsq_ready, 1)

            def tanh_z(u):
                act_e.wait_ge(z_ready, u + 1)
                if u in REUSES:
                    act_e.wait_ge(aT_ready, u)
                t = tokens(u)
                act_e.activation(th[:, t], z[:, t], ACT.Tanh, scale=GELU_C * GELU_A).then_inc(th_ready, 1)

            def split_x_hi(u):
                b = UNITS[u][0]
                act_e.wait_ge(xnT_done[1], u + 1)
                if b >= 2:
                    act_e.wait_ge(u_done, KB * (b - 1))
                    act_e.wait_ge(logits_done, b - 1)
                t = tokens(u)
                act_e.activation(xh[:, b % 2, t], side_t(u)[:, t], ACT.Copy).then_inc(xh_ready, 1)

            def tanh_logits(b):
                act_e.wait_ge(lg_ready, b + 1)
                if b:
                    act_e.wait_ge(r_step, R_ALL * (b - 1) + 1)
                act_e.activation(rth[:], lg[:], ACT.Tanh, scale=0.5).then_inc(rth_ready, 1)

            def evac_combT(b):
                act_e.wait_ge(combT_done, b + 1)
                if b:
                    act_e.wait_ge(comb_out, 16 * b)
                act_e.activation(combT[:], bank_l[0:J * E, 0:P], ACT.Copy).then_inc(combT_ready, 1)

            def silu(i):
                act_e.wait_ge(g_done, i + 1)
                if i >= 3:
                    act_e.wait_ge(act_ready, i - 2)
                act_e.activation(sg[:, i % 3], bank_g[i % 2][:], ACT.Silu).then_inc(sg_ready, 1)

            def split_act_hi(d):
                if place(d)[1]:
                    act_e.wait_ge(act_scaled, scaled_before(d))
                else:
                    act_e.wait_ge(act_ready, d + 1)
                if d >= 2:
                    act_e.wait_ge(down_done, d - 1)
                act_e.activation(ah[:, d % 2], act[:, d % RING], ACT.Copy).then_inc(ah_ready, 1)

            def evac_y(v):
                b, j0, j1 = OUTS[v]
                act_e.wait_ge(down_done, KB * (b + 1))
                if v:
                    act_e.wait_ge(yT_done, b)
                t = slice(j0 * P, j1 * P)
                act_e.activation(yT[:, t], bank_y[:, t], ACT.Copy, scale=gates_t[:, 1:2]).then_inc(y_ready, 1)

            for t in range(FIRST, LAST):
                for i in slot_at(t, SILU_AT):
                    if i < SLOTS:
                        silu(i)
                for u in now("norm1", t):
                    normalise(u, 0)
                for _ in now("ctxT", t):
                    evac_ctxT()
                for u in now("xnT", t):
                    evac_xnT(u)
                for u in now("square", t):
                    square_h(u)
                for u in now("tanh", t):
                    tanh_z(u)
                for u in now("norm2", t):
                    normalise(u, 1)
                for u in now("x_hi", t):
                    split_x_hi(u)
                for _ in now("small", t):
                    small_inputs()
                for b in now("logits", t):
                    tanh_logits(b)
                for b in now("combT", t):
                    evac_combT(b)
                for v in now("y", t):
                    evac_y(v)
                for k in now("w_hi", t):
                    split_hi(k)
                for i in slot_at(t, HI_AT):
                    for d in DOWNS[min(i + 1, SLOTS)] if i < SLOTS else []:
                        if d not in WHOLE:
                            split_act_hi(d)

        @block.vector
        def _(dve):
            norms = []

            def layer_stats(u, n):
                b, j0, j1 = UNITS[u]
                if n == 0:
                    dve.wait_ge(x_in[u], 16)
                else:
                    dve.wait_ge(x2_ready, u + 1)
                if norms and u in REUSES:
                    v, m = norms[-1]
                    dve.wait_ge(mv_ready[m], J * UNITS[v][0] + UNITS[v][2])
                for j in range(j0, j1):
                    dve.bn_stats(stats[:, n, j], xt[:, b, j]).then_inc(stats_done, 1)
                if u in REUSES:
                    dve.wait_ge(rstd_ready[n], u)
                    if u > REUSES[0]:
                        dve.wait_ge(nmr_ready[n], u - REUSES[0])
                    else:
                        dve.wait_ge(xn_first[n], J)
                done = sum(UNITS[v][2] - UNITS[v][1] for v, _ in norms)
                for j in range(j0, j1):
                    dve.wait_ge(stats_done, done + j - j0 + 1)
                    dve.bn_aggr(mv[:, n, j], stats[:, n, j]).then_inc(mv_ready[n], 1)
                norms.append((u, n))

            def normalise(u, n):
                b, j0, j1 = UNITS[u]
                dve.wait_ge(rstd_ready[n], u + 1)
                dve.wait_ge(mv_ready[n], J * b + j1)
                for j in range(j0, j1):
                    dve.tensor_scalar(xn[:, n, j], xt[:, b, j], mv[:, n, j, 0:1], rstd[:, n, j:j + 1],
                                      ALU.subtract, ALU.mult).then_inc(xn_first[n], 1)

            def gelu_z(u):
                dve.wait_ge(hsq_ready, u + 1)
                if u in REUSES:
                    dve.wait_ge(th_ready, u)
                t = tokens(u)
                dve.scalar_tensor_tensor(z[:, t], hsq[:, t], 1.0 / GELU_A, side_h(u)[0:C, t], ALU.add, ALU.mult).then_inc(z_ready, 1)

            def gelu_a(u):
                dve.wait_ge(th_ready, u + 1)
                if u in REUSES:
                    dve.wait_ge(attn_done, u)
                t = tokens(u)
                dve.scalar_tensor_tensor(aT[:, t], th[:, t], 1.0, side_h(u)[0:C, t], ALU.add, ALU.mult).then_inc(aT_ready, 1)

            def residual(u):
                b, j0, j1 = UNITS[u]
                dve.wait_ge(attn_done, u + 1)
                dve.wait_ge(gates_ready, 1)
                if u in REUSES:
                    dve.wait_ge(xn_ready[0], J * b)
                dve.scalar_tensor_tensor(xt[:, b, j0:j1], side_h(u)[:, tokens(u)].rearrange("p (j h) -> p j h", h=H), gx_half[:, 0:1],
                                         xt[:, b, j0:j1], ALU.mult, ALU.add).then_inc(x2_ready, 1)

            def split_x_lo(u):
                b, t = UNITS[u][0], tokens(u)
                dve.wait_ge(xh_ready, u + 1)
                dve.tensor_tensor(xl[:, b % 2, t], side_t(u)[:, t], xh[:, b % 2, t].bitcast(F32), ALU.subtract).then_inc(xl_ready, 1)

            def router(b, n):
                done = R_ALL * b + sum(R_OPS[:n])
                if done and n:
                    dve.wait_ge(r_step, done)
                masked_v = masked[:].rearrange("p j e -> p (j e)").rearrange("p (g e) -> p g e", e=EG)
                sfc_v = sfc[:].rearrange("p j e -> p (j e)").rearrange("p (g e) -> p g e", e=EG)
                pairs = sfc[:].rearrange("p j e -> p (j e)").rearrange("p (q r) -> p r q", r=2)
                if n == 0:
                    dve.wait_ge(logits_done, b + 1)
                    if b:
                        dve.wait_ge(rth_ready, b)
                    dve.tensor_reduce(lg[:].rearrange("p (j e) -> p j e", j=J),
                                      bank_l[:, 0:J * 2 * E].rearrange("p (j s e) -> p j e s", j=J, s=2), AX.X, ALU.add).then_inc(lg_ready, 1)
                elif n == 1:
                    dve.wait_ge(rth_ready, b + 1)
                    dve.scalar_tensor_tensor(sfc[:, :, 0:E], rth[:].rearrange("p (j e) -> p j e", j=J), 0.5,
                                             bias_h[:].unsqueeze(1).broadcast_to([P, J, E]), ALU.mult, ALU.add).then_inc(r_step, 1)
                elif n == 2:
                    dve.tensor_tensor(pmax[:], pairs[:, 0], pairs[:, 1], ALU.max).then_inc(r_step, 1)
                    dve.tensor_tensor(pmin[:], pairs[:, 0], pairs[:, 1], ALU.min).then_inc(r_step, 1)
                elif n == 3:
                    mx = pmax[:].rearrange("p (q r) -> p r q", r=2)
                    mn = pmin[:].rearrange("p (q r) -> p r q", r=2)
                    dve.tensor_tensor(top[:], mx[:, 0], mx[:, 1], ALU.max).then_inc(r_step, 1)
                    dve.tensor_tensor(sec_a[:], mx[:, 0], mx[:, 1], ALU.min).then_inc(r_step, 1)
                    dve.tensor_tensor(sec_b[:], mn[:, 0], mn[:, 1], ALU.max).then_inc(r_step, 1)
                elif n == 4:
                    dve.tensor_tensor(sec[:], sec_a[:], sec_b[:], ALU.max).then_inc(r_step, 1)
                elif n == 5:
                    dve.tensor_tensor(gs[:].rearrange("p j g -> p (j g)"), top[:], sec[:], ALU.add).then_inc(r_step, 1)
                elif n == 6:
                    other = gs[:, :, 0:NG].unsqueeze(2).broadcast_to([P, J, NG, NG])
                    own = gs[:, :, 0:NG].unsqueeze(3).broadcast_to([P, J, NG, NG])
                    dve.tensor_tensor(gt[:], other, own, ALU.is_gt).then_inc(r_step, 1)
                    dve.tensor_tensor(eq[:], other, own, ALU.is_equal).then_inc(r_step, 1)
                elif n == 7:
                    dve.tensor_tensor(eq[:], eq[:], before[:].unsqueeze(1).broadcast_to([P, J, NG, NG]), ALU.mult).then_inc(r_step, 1)
                elif n == 8:
                    dve.tensor_tensor(gt[:], gt[:], eq[:], ALU.add).then_inc(r_step, 1)
                elif n == 9:
                    dve.tensor_reduce(rank[:, :, 0:NG], gt[:], AX.X, ALU.add).then_inc(r_step, 1)
                elif n == 10:
                    dve.scalar_tensor_tensor(masked_v, rank[:].rearrange("p j g -> p (j g)").unsqueeze(2).broadcast_to([P, J * (NG + 1), EG]),
                                             float(TOPG), sfc_v, ALU.is_lt, ALU.mult).then_inc(r_step, 1)
                elif n == 11:
                    for j in range(J):
                        dve.max(top8[:, j], masked[:, j]).then_inc(r_step, 1)
                elif n == 12:
                    for j in range(J):
                        dve.match_replace(rep[:, j], top8[:, j], masked[:, j], PICKED).then_inc(r_step, 1)
                    dve.tensor_reduce(den[:], top8[:, :, EG:EG + TOPK], AX.X, ALU.add).then_inc(r_step, 1)
                elif n == 13:
                    dve.tensor_scalar(den2[:], den[:], 1e-20, 1.0 / ROUTE_SCALE, ALU.add, ALU.mult).then_inc(r_step, 1)
                    dve.scalar_tensor_tensor(num[:], rep[:, :, 0:E], PICKED, masked[:, :, 0:E], ALU.is_equal, ALU.mult).then_inc(r_step, 1)
                elif n == 14:
                    dve.reciprocal(rec[:], den2[:]).then_inc(r_step, 1)
                elif n == 15:
                    if b:
                        dve.wait_ge(combT_done, b)
                    dve.tensor_tensor(comb[:].rearrange("p e j -> p j e"), num[:], rec[:].unsqueeze(2).broadcast_to([P, J, E]), ALU.mult).then_inc(r_step, 1)

            def gate_up(i):
                dve.wait_ge(sg_ready, i + 1)
                dve.wait_ge(u_done, i + 1)
                if i >= RING:
                    dve.wait_ge(al_ready, i - RING + 1)
                dve.tensor_tensor(act[:, i % RING], sg[:, i % 3], bank_u[i % 2][:], ALU.mult).then_inc(act_ready, 1)

            def split_act_lo(d):
                dve.wait_ge(ah_ready, d + 1)
                dve.tensor_tensor(al[:, d % 2], act[:, d % RING], ah[:, d % 2].bitcast(F32), ALU.subtract).then_inc(al_ready, 1)

            def finish(v):
                b, j0, j1 = OUTS[v]
                dve.wait_ge(yT_done, v + 1)
                if b >= 2:
                    dve.wait_ge(out_done, 16 * (b - 1))
                dve.tensor_tensor(ot[:, b % 2, j0:j1], side_y(v)[:, j0 * H:j1 * H].rearrange("p (j h) -> p j h", h=H),
                                  xt[:, b, j0:j1], ALU.add).then_inc(ot_ready, 1)

            dve.memset(sfc[:], BIG).then_inc(sentinels, 1)
            dve.memset(rank[:], 0.0).then_inc(sentinels, 1)
            dve.memset(warm[:], 0.0).then_inc(warm_ready, 1)
            dve.wait_ge(sentinels, 2)
            for t in range(FIRST, LAST):
                for _ in now("small_dve", t):
                    dve.wait_ge(gates_tanh, 1)
                    dve.tensor_scalar(gx_half[:], gates_t[:, 0:1], 0.5, None, ALU.mult).then_inc(gates_ready, 1)
                    dve.tensor_scalar(bias_h[:], bias_b[:], 0.5, None, ALU.add).then_inc(bias_ready, 1)
                    dve.wait_ge(bias_ready, 1)
                for i in slot_at(t, MUL_AT):
                    if i < SLOTS:
                        gate_up(i)
                for i in slot_at(t, LO_AT):
                    for d in DOWNS[min(i + 1, SLOTS)] if i < SLOTS else []:
                        if d not in WHOLE:
                            split_act_lo(d)
                for u in now("residual", t):
                    residual(u)
                for u in now("x_lo", t):
                    split_x_lo(u)
                for u in now("stats2", t):
                    layer_stats(u, 1)
                for u in now("norm2_dve", t):
                    normalise(u, 1)
                for u in now("z", t):
                    gelu_z(u)
                for u in now("a", t):
                    gelu_a(u)
                for u in now("stats1", t):
                    layer_stats(u, 0)
                for u in now("norm1_dve", t):
                    normalise(u, 0)
                for v in now("finish", t):
                    finish(v)
                for b in range(NB):
                    for n in router_steps(b, t):
                        router(b, n)

        @block.tensor
        def _(pe):
            reader = {"t": None, "h": None, "t1": None, "h1": None, "y": None, "l": (ctxT_ready, 1)}

            def free(bank):
                if reader[bank]:
                    pe.wait_ge(*reader[bank])

            def warm_up(n):
                for _ in range(n):
                    pe.matmul(bank_y[:, 0:P], ident[:], ident[:], start=True, stop=True)

            def transpose_xn(u, n):
                b, j0, j1 = UNITS[u]
                pe.wait_ge(*((xn_ready[n], J * b) if u in REUSES else (xn_first[n], j1)))
                bank = "t1" if u == 1 else "t"
                free(bank)
                for j in range(j0, j1):
                    last = pe.transpose(side_t(u)[:, j * P:(j + 1) * P], xn[:, n, j], ident[:])
                last.then_inc(xnT_done[n], 1)
                reader[bank] = (xl_ready if n else xnT_ready, u + 1)

            def hidden(u):
                b, t = UNITS[u][0], tokens(u)
                pe.wait_ge(xnT_ready, u + 1)
                bank = "h1" if u == 1 else "h"
                free(bank)
                pe.matmul(side_h(u)[0:C, t], ctxT[:, b], xnT[:, t], start=True, stop=True).then_inc(h_done, 1)
                reader[bank] = (aT_ready, u + 1)

            def attend(u):
                b, j0, j1 = UNITS[u]
                pe.wait_ge(aT_ready, u + 1)
                for j in range(j0, j1):
                    last = pe.matmul(side_h(u)[:, j * H:(j + 1) * H], aT[:, j * P:(j + 1) * P], ctx_sb[:, b], start=True, stop=True)
                last.then_inc(attn_done, 1)
                reader["h1" if u == 1 else "h"] = (x2_ready, u + 1)

            def logits(b):
                pe.wait_ge(xl_ready, LAST_UNIT[b] + 1)
                free("l")
                for j in range(J):
                    o = bank_l[:, 2 * E * j:2 * E * (j + 1)]
                    t = slice(j * P, (j + 1) * P)
                    parts = gk_parts[:].rearrange("p s e -> p (s e)")
                    pe.matmul(o, xh[:, b % 2, t], parts, start=True, stop=False)
                    last = pe.matmul(o, xl[:, b % 2, t], parts, start=False, stop=True)
                last.then_inc(logits_done, 1)
                reader["l"] = (lg_ready, b + 1)

            def transpose_comb(b):
                pe.wait_ge(r_step, R_ALL * (b + 1))
                free("l")
                pe.transpose(bank_l[0:J * E, 0:P], comb[:].rearrange("p e j -> p (e j)"), ident[:]).then_inc(combT_done, 1)
                reader["l"] = (combT_ready, b + 1)

            def three(o, k, i, hi, lo, start, stop):
                pe.matmul(o, w_lo[:, k, i], hi, start=start, stop=False)
                pe.matmul(o, w_hi[:, k, i], hi, start=False, stop=False)
                return pe.matmul(o, w_hi[:, k, i], lo, start=False, stop=stop)

            def gate_up(i):
                b, k = place(i)
                if i % KB == 0 and b:
                    pe.wait_ge(xl_ready, LAST_UNIT[b] + 1)
                if b == 0:
                    pe.wait_ge(w_lo_ready, k + 1)
                if i >= 2:
                    pe.wait_ge(act_ready, i - 1)
                hi, lo = xh[:, b % 2], xl[:, b % 2]
                if i == 0:
                    for u in range(2):
                        t = tokens(u)
                        pe.wait_ge(xl_ready, u + 1)
                        gate = three(bank_g[0][:, t], k, 0, hi[:, t], lo[:, t], True, True)
                        if u == 1:
                            gate.then_inc(g_done, 1)
                        up = three(bank_u[0][:, t], k, 1, hi[:, t], lo[:, t], True, True)
                    up.then_inc(u_done, 1)
                    return
                three(bank_g[i % 2][:], k, 0, hi, lo, True, True).then_inc(g_done, 1)
                three(bank_u[i % 2][:], k, 1, hi, lo, True, True).then_inc(u_done, 1)

            def down(d):
                b, k = place(d)
                first, last = d % KB == 0, d % KB == KB - 1
                if first:
                    free("y")
                if d in WHOLE:
                    if k:
                        pe.wait_ge(act_scaled, scaled_before(d))
                    else:
                        pe.wait_ge(act_ready, d + 1)
                    pe.matmul(bank_y[:], w_raw[:, k, 2], act[:, d % RING], start=first, stop=last).then_inc(down_done, 1)
                else:
                    pe.wait_ge(al_ready, d + 1)
                    three(bank_y[:], k, 2, ah[:, d % 2], al[:, d % 2], first, last).then_inc(down_done, 1)
                reader["y"] = (y_ready, b + 1)

            def transpose_y(v):
                _, j0, j1 = OUTS[v]
                bank = "th"[v == len(OUTS) - 1]
                pe.wait_ge(y_ready, v + 1)
                free(bank)
                for j in range(j0, j1):
                    last = pe.transpose(side_y(v)[:, j * H:(j + 1) * H], yT[:, j * P:(j + 1) * P], ident[:])
                last.then_inc(yT_done, 1)
                reader[bank] = (ot_ready, v + 1)

            def transpose_ctx():
                pe.wait_ge(ctx_in_s, 16)
                for b in range(NB):
                    last = pe.transpose(bank_l[:, b * C:(b + 1) * C], ctx_sb[:, b], ident[0:C, 0:C])
                last.then_inc(ctxT_done, 1)

            pe.wait_ge(const_ready, 3)
            warm_up(WARM_UP)
            for t in range(FIRST, LAST):
                warm_up(len(now("keep_warm", t)))
                for i in slot_at(t, GATE_UP_AT):
                    if i < SLOTS:
                        gate_up(i)
                for _ in now("ctxT", t):
                    transpose_ctx()
                for u in now("T1", t):
                    transpose_xn(u, 0)
                for u in now("h", t):
                    if u == 0:
                        pe.wait_ge(ctxT_ready, 1)
                    hidden(u)
                for u in now("attend", t):
                    attend(u)
                for u in now("T2", t):
                    transpose_xn(u, 1)
                for b in now("logits_pe", t):
                    if b == 0:
                        pe.wait_ge(gk_lo_ready, 1)
                    logits(b)
                for b in now("combT_pe", t):
                    transpose_comb(b)
                for v in now("yT", t):
                    transpose_y(v)
                for i in slot_at(t, DOWN_AT):
                    for d in DOWNS[i]:
                        down(d)


_INS = ['x', 'ctx_1024', 'g_xattn', 'g_ffn', 'L0_ffn_gate_kernel', 'L0_ffn_gate_bias', 'L0_ffn_w_gate', 'L0_ffn_w_up',
        'L0_ffn_w_down', 'L0_ffn_sw_gate', 'L0_ffn_sw_up', 'L0_ffn_sw_down']


def kernel(**inputs):
    import numpy as _np
    import concourse.bacc as _bacc
    from concourse import mybir as _mybir
    from concourse.bass_utils import run_bass_kernel_spmd as _run

    nc = _bacc.Bacc("TRN2", target_bir_lowering=False, num_devices=1)
    arrays, args = {}, []
    for name in _INS:
        a = _np.ascontiguousarray(inputs[name])
        arrays[f"in_{name}_dram"] = a
        args.append(nc.dram_tensor(f"in_{name}_dram", a.shape, _mybir.dt.from_np(a.dtype), kind="ExternalInput").ap())
    args.append(nc.dram_tensor("combine_weights", (NB, E, S), F32, kind="Internal").ap())
    args.append(nc.dram_tensor("out_0_dram", (NB, S, H), F32, kind="ExternalOutput").ap())
    flamingo_block(nc, *args)
    r = _run(nc, [arrays], core_ids=[0])
    return r.results[0]["out_0_dram"]
```
